# Optimizing a Trainium2 kernel written in Bass

```python
import numpy as np
import jax
import jax.numpy as jnp

def _softmax(x, axis=-1):
    return jax.nn.softmax(x, axis=axis)

def _gelu(x):
    return jax.nn.gelu(x, approximate=True)

def _silu(x):
    return jax.nn.silu(x)

def _sigmoid(x):
    return jax.nn.sigmoid(x)

def _layernorm(x, axis=-1, eps=1e-05):
    m = jnp.mean(x, axis=axis, keepdims=True)
    v = jnp.var(x, axis=axis, keepdims=True)
    return (x - m) / jnp.sqrt(v + eps)

def _scatter_add(tgt, idx, src, axis=0):
    return tgt.at[idx].add(src)

def _segment_sum(src, seg, n):
    return jax.ops.segment_sum(src, seg, n)
kernel_name = 'mk_adj_preln_d4_adj_r2_c59c73'

def setup_inputs(seed: int=0):
    np.random.seed(seed)
    _w = jnp.asarray

    def _rec_inputs():
        import jax
        import jax.numpy as jnp
        _gk = jax.random.key(seed)
        x = -0.0005207 + 1.001 * jax.random.normal(jax.random.fold_in(_gk, 1), (64, 128, 128), jnp.float32)
        _a = jax.random.bernoulli(jax.random.fold_in(_gk, 2), 0.03125, (64, 128, 128))
        _a = jnp.logical_or(_a, jnp.swapaxes(_a, -1, -2))
        _a = jnp.logical_or(_a, jnp.eye(128, dtype=bool))
        adj = _a.astype(jnp.int32)
        _nm = jnp.ones((64, 128), dtype=bool)
        nodemask = jnp.where(_nm, 1.0, 0.0).astype(jnp.float32)
        return (x, adj, nodemask)
    x, adj, nodemask = _rec_inputs()

    def _L0_gnn_setup():
        import jax, jax.numpy as jnp
        import numpy as np
        B, N, F_IN, F_OUT = (8, 1024, 128, 128)
        NEG_BIG = -9000000000000000.0
        LEAKY_SLOPE = 0.01
        key = jax.random.key(seed)
        k1, k2, k3, k4, k5 = jax.random.split(key, 5)
        features = jax.random.normal(k1, (B, N, F_IN), dtype=jnp.float32)
        adj_matrix = jax.random.randint(k2, (B, N, N), 0, 2, dtype=jnp.int32)
        mask = jnp.ones((B, N), dtype=jnp.float32)
        W = jax.random.normal(k3, (F_IN, F_OUT), dtype=jnp.float32) / np.sqrt(F_IN)
        b = jnp.zeros((F_OUT,), dtype=jnp.float32)
        a = jax.random.normal(k4, (2 * F_OUT,), dtype=jnp.float32) / np.sqrt(2 * F_OUT)
        return {'features': features, 'adj_matrix': adj_matrix, 'mask': mask, 'W': W, 'b': b, 'a': a}
    _L0_gnn_all = _L0_gnn_setup()
    _L0_gnn_in = {k: v for k, v in _L0_gnn_all.items() if k in ('W', 'b', 'a')}
    del _L0_gnn_all

    def _L1_gnn_setup():
        import jax, jax.numpy as jnp
        import numpy as np
        B, K, Z, H = (16, 128, 128, 128)
        key = jax.random.key(seed)
        ks = jax.random.split(key, 8)
        z = jax.random.normal(ks[0], (B, K, Z), dtype=jnp.float32)
        P = jax.random.randint(ks[1], (B, K, K), 0, 2, dtype=jnp.int32)
        P = jnp.clip(P + jnp.eye(K, dtype=jnp.int32)[None], 0, 1)
        s = 1.0 / np.sqrt(Z)
        su = 1.0 / np.sqrt(2 * Z)
        W1 = jax.random.uniform(ks[2], (Z, Z), jnp.float32, -s, s)
        b1 = jax.random.uniform(ks[3], (Z,), jnp.float32, -s, s)
        W2 = jax.random.uniform(ks[4], (Z, Z), jnp.float32, -s, s)
        b2 = jax.random.uniform(ks[5], (Z,), jnp.float32, -s, s)
        Wu = jax.random.uniform(ks[6], (H, 2 * Z), jnp.float32, -su, su)
        bu = jax.random.uniform(ks[7], (H,), jnp.float32, -su, su)
        return {'z': z, 'P': P, 'W1': W1, 'b1': b1, 'W2': W2, 'b2': b2, 'Wu': Wu, 'bu': bu}
    _L1_gnn_all = _L1_gnn_setup()
    _L1_gnn_in = {k: v for k, v in _L1_gnn_all.items() if k in ('W1', 'b1', 'W2', 'b2', 'Wu', 'bu')}
    del _L1_gnn_all

    def _L2_gnn_setup():
        import jax, jax.numpy as jnp
        import numpy as np
        B, D, FIN, FOUT, H = (16, 256, 128, 128, 8)
        NEG_INF = -9000000000000000.0
        key = jax.random.key(seed)
        k1, k2, k3, k4, k5 = jax.random.split(key, 5)
        x = jax.random.normal(k1, (B, D, FIN), dtype=jnp.float32)
        adj = jax.random.randint(k2, (B, D, D), 0, 2, dtype=jnp.int32)
        limW = float(np.sqrt(6.0 / (FIN + FOUT))) * 1.414
        W = jax.random.uniform(k3, (FIN, FOUT), minval=-limW, maxval=limW, dtype=jnp.float32)
        lima = float(np.sqrt(6.0 / (2 * FOUT + H))) * 1.414
        a_w = jax.random.uniform(k4, (H, 2 * FOUT), minval=-lima, maxval=lima, dtype=jnp.float32)
        a_b = jax.random.uniform(k5, (H,), minval=-0.05, maxval=0.05, dtype=jnp.float32)
        return {'input': x, 'adj': adj, 'W': W, 'a_w': a_w, 'a_b': a_b}
    _L2_gnn_all = _L2_gnn_setup()
    _L2_gnn_in = {k: v for k, v in _L2_gnn_all.items() if k in ('W', 'a_w', 'a_b')}
    del _L2_gnn_all

    def _L3_gnn_setup():
        import jax, jax.numpy as jnp
        import numpy as np
        EPS = 1e-05
        NEG = jnp.float32(-9000000000000000.0)

        def _leaky(z):
            return jnp.where(z >= 0, z, 0.01 * z)
        key = jax.random.key(seed)
        ks = jax.random.split(key, 12)
        B, N, d_in, d_hid, d_out = (4, 256, 128, 128, 128)
        d_mid = d_in // 2
        s = lambda fan: 1.0 / np.sqrt(fan)
        inp = {'x': jax.random.normal(ks[0], (B, N, d_in), dtype=jnp.float32), 'A_init': jax.random.randint(ks[1], (B, N, N), 0, 2, dtype=jnp.int32), 'W1': jax.random.normal(ks[2], (d_mid, d_in), dtype=jnp.float32) * s(d_in), 'b1': jnp.zeros((d_mid,), dtype=jnp.float32), 'g1': jnp.ones((d_mid,), dtype=jnp.float32), 'be1': jnp.zeros((d_mid,), dtype=jnp.float32), 'W2': jax.random.normal(ks[3], (1, d_mid), dtype=jnp.float32) * s(d_mid), 'b2': jnp.zeros((1,), dtype=jnp.float32), 'Wg': jax.random.normal(ks[4], (d_hid, d_in), dtype=jnp.float32) * s(d_in), 'bg': jnp.zeros((d_hid,), dtype=jnp.float32), 'gg': jnp.ones((d_hid,), dtype=jnp.float32), 'beg': jnp.zeros((d_hid,), dtype=jnp.float32), 'Wt': jax.random.normal(ks[5], (d_out, d_in + d_hid), dtype=jnp.float32) * s(d_in + d_hid), 'bt': jnp.zeros((d_out,), dtype=jnp.float32)}
        return inp
    _L3_gnn_all = _L3_gnn_setup()
    _L3_gnn_in = {k: v for k, v in _L3_gnn_all.items() if k in ('W1', 'b1', 'g1', 'be1', 'W2', 'b2', 'Wg', 'bg', 'gg', 'beg', 'Wt', 'bt')}
    del _L3_gnn_all
    return {'x': x, 'adj': adj, 'nodemask': nodemask, 'L0_gnn_W': _L0_gnn_in['W'], 'L0_gnn_b': _L0_gnn_in['b'], 'L0_gnn_a': _L0_gnn_in['a'], 'L1_gnn_W1': _L1_gnn_in['W1'], 'L1_gnn_b1': _L1_gnn_in['b1'], 'L1_gnn_W2': _L1_gnn_in['W2'], 'L1_gnn_b2': _L1_gnn_in['b2'], 'L1_gnn_Wu': _L1_gnn_in['Wu'], 'L1_gnn_bu': _L1_gnn_in['bu'], 'L2_gnn_W': _L2_gnn_in['W'], 'L2_gnn_a_w': _L2_gnn_in['a_w'], 'L2_gnn_a_b': _L2_gnn_in['a_b'], 'L3_gnn_W1': _L3_gnn_in['W1'], 'L3_gnn_b1': _L3_gnn_in['b1'], 'L3_gnn_g1': _L3_gnn_in['g1'], 'L3_gnn_be1': _L3_gnn_in['be1'], 'L3_gnn_W2': _L3_gnn_in['W2'], 'L3_gnn_b2': _L3_gnn_in['b2'], 'L3_gnn_Wg': _L3_gnn_in['Wg'], 'L3_gnn_bg': _L3_gnn_in['bg'], 'L3_gnn_gg': _L3_gnn_in['gg'], 'L3_gnn_beg': _L3_gnn_in['beg'], 'L3_gnn_Wt': _L3_gnn_in['Wt'], 'L3_gnn_bt': _L3_gnn_in['bt']}

def reference(x, adj, nodemask, L0_gnn_W, L0_gnn_b, L0_gnn_a, L1_gnn_W1, L1_gnn_b1, L1_gnn_W2, L1_gnn_b2, L1_gnn_Wu, L1_gnn_bu, L2_gnn_W, L2_gnn_a_w, L2_gnn_a_b, L3_gnn_W1, L3_gnn_b1, L3_gnn_g1, L3_gnn_be1, L3_gnn_W2, L3_gnn_b2, L3_gnn_Wg, L3_gnn_bg, L3_gnn_gg, L3_gnn_beg, L3_gnn_Wt, L3_gnn_bt):
    import jax
    import jax.numpy as jnp

    def _L0_gnn_ref(features, adj_matrix, mask, W, b, a):
        import jax, jax.numpy as jnp
        import numpy as np
        B, N, F_IN, F_OUT = (8, 1024, 128, 128)
        NEG_BIG = -9000000000000000.0
        LEAKY_SLOPE = 0.01
        h = jnp.einsum('bni,io->bno', features, W) + b
        a_src, a_dst = (a[:F_OUT], a[F_OUT:])
        e = (h @ a_src)[:, :, None] + (h @ a_dst)[:, None, :]
        e = jnp.where(e >= 0, e, LEAKY_SLOPE * e)
        scores = jnp.where(adj_matrix > 0, e, jnp.float32(NEG_BIG))
        attention = jax.nn.softmax(scores, axis=-1)
        aggregated = jnp.einsum('bnm,bmo->bno', attention, h)
        aggregated = aggregated * mask[:, :, None]
        return aggregated

    def _L1_gnn_ref(z, P, W1, b1, W2, b2, Wu, bu):
        import jax, jax.numpy as jnp
        import numpy as np
        B, K, Z, H = (16, 128, 128, 128)
        m1z = z @ W1.T + b1
        m2z = z @ W2.T + b2
        pair = jax.nn.relu(m1z[:, :, None, :] + m2z[:, None, :, :])
        mask = (jnp.swapaxes(P, 1, 2) != 0)[..., None]
        m = jnp.max(jnp.where(mask, pair, -jnp.inf), axis=2)
        return jax.nn.relu(jnp.concatenate((z, m), axis=-1) @ Wu.T + bu)

    def _L2_gnn_ref(input, adj, W, a_w, a_b):
        import jax, jax.numpy as jnp
        import numpy as np
        B, D, FIN, FOUT, H = (16, 256, 128, 128, 8)
        NEG_INF = -9000000000000000.0
        h = input @ W
        F = h.shape[-1]
        a1, a2 = (a_w[:, :F], a_w[:, F:])
        s1 = jnp.einsum('bif,hf->bhi', h, a1)
        s2 = jnp.einsum('bjf,hf->bhj', h, a2)
        e = jax.nn.leaky_relu(s1[:, :, :, None] + s2[:, :, None, :] + a_b[None, :, None, None])
        att = jnp.where(adj[:, None, :, :] > 0, e, NEG_INF)
        att = jax.nn.softmax(att, axis=-1)
        h_prime = jnp.einsum('bhij,bjf->bif', att, h) / att.shape[1]
        return h_prime

    def _L3_gnn_ref(x, A_init, W1, b1, g1, be1, W2, b2, Wg, bg, gg, beg, Wt, bt):
        import jax, jax.numpy as jnp
        import numpy as np
        EPS = 1e-05
        NEG = jnp.float32(-9000000000000000.0)

        def _leaky(z):
            return jnp.where(z >= 0, z, 0.01 * z)
        D = jnp.abs(x[:, :, None, :] - x[:, None, :, :])
        h = jnp.einsum('bijc,oc->bijo', D, W1) + b1
        m = jnp.mean(h, axis=(0, 1, 2))
        v = jnp.mean((h - m) ** 2, axis=(0, 1, 2))
        h = (h - m) / jnp.sqrt(v + EPS) * g1 + be1
        h = _leaky(h)
        s = jnp.einsum('bijo,uo->biju', h, W2)[..., 0] + b2[0]
        s = jnp.where(A_init > 0, s, NEG)
        A = jax.nn.softmax(s, axis=-1)
        y = jnp.einsum('bij,bjc->bic', A, x)
        y = y @ Wg.T + bg
        mg = jnp.mean(y, axis=(0, 1))
        vg = jnp.mean((y - mg) ** 2, axis=(0, 1))
        y = (y - mg) / jnp.sqrt(vg + EPS) * gg + beg
        y = _leaky(y)
        out = jnp.concatenate([x, y], axis=2) @ Wt.T + bt
        return out
    h = jnp.maximum(_layernorm(x, axis=-1), 0.0)
    x = x + _L0_gnn_ref(h, adj, nodemask, L0_gnn_W, L0_gnn_b, L0_gnn_a)
    h = jnp.maximum(_layernorm(x, axis=-1), 0.0)
    x = x + _L1_gnn_ref(h, adj, L1_gnn_W1, L1_gnn_b1, L1_gnn_W2, L1_gnn_b2, L1_gnn_Wu, L1_gnn_bu)
    h = jnp.maximum(_layernorm(x, axis=-1), 0.0)
    x = x + _L2_gnn_ref(h, adj, L2_gnn_W, L2_gnn_a_w, L2_gnn_a_b)
    h = jnp.maximum(_layernorm(x, axis=-1), 0.0)
    x = x + _L3_gnn_ref(h, adj, L3_gnn_W1, L3_gnn_b1, L3_gnn_g1, L3_gnn_be1, L3_gnn_W2, L3_gnn_b2, L3_gnn_Wg, L3_gnn_bg, L3_gnn_gg, L3_gnn_beg, L3_gnn_Wt, L3_gnn_bt)
    return x

_drawn_inputs = setup_inputs


def setup_inputs(seed=0):
    import zlib

    import numpy as np

    out = dict(_drawn_inputs(seed))
    spreads = {'L0_gnn_b': (0.0, 0.1),
     'L3_gnn_b1': (0.0, 2.0),
     'L3_gnn_g1': (1.0, 0.6),
     'L3_gnn_be1': (0.0, 0.609),
     'L3_gnn_bg': (0.0, 2.0),
     'L3_gnn_gg': (1.0, 0.2),
     'L3_gnn_beg': (0.0, 0.281),
     'L3_gnn_bt': (0.0, 0.1)}
    factors = {'L1_gnn_b1': 4.892, 'L1_gnn_b2': 4.446, 'L2_gnn_a_b': 55.442}
    for name, (base, spread) in spreads.items():
        noise = np.random.default_rng([zlib.crc32(name.encode()), seed]).standard_normal(out[name].shape)
        drawn = base * np.exp(spread * noise) if base else spread * noise
        out[name] = jnp.asarray(drawn.astype(out[name].dtype))
    for name, factor in factors.items():
        out[name] = (out[name] * factor).astype(out[name].dtype)
    return out
```

```python
from contextlib import ExitStack

import numpy as np
import concourse.bass as bass
from concourse import mybir

ALU = mybir.AluOpType
ACT = mybir.ActivationFunctionType
F32 = mybir.dt.float32
BF16 = mybir.dt.bfloat16
I32 = mybir.dt.int32
AX = mybir.AxisListType

B, N, C = 64, 128, 128
G = 4
QUADS = B // G
QC = G * N
EPS = 1e-5
BIG = float(2.0 ** 60)
LOWEST = -3.0e38
HEADS = 8
BLK = 6
NBLK = (N + BLK - 1) // BLK
SUB = 2 ** BLK
NCH = NBLK // 2
NG = (NCH + 3) // 4
HID = C // 2
BIAS = 8


def done(n):
    return n + 1 + BIAS


def constants():
    bf = mybir.dt.np(BF16)
    subset = np.arange(SUB)
    sel = np.zeros((N, NBLK * SUB), np.float32)
    for j in range(N):
        blk, t = divmod(j, BLK)
        sel[j, blk * SUB:(blk + 1) * SUB] = 2.0 * ((subset >> t) & 1) - 1.0
    nhot = 1.0 - sum((subset >> t) & 1 for t in range(BLK))
    blockind = np.zeros((HEADS, HEADS * N), np.float32)
    for h in range(HEADS):
        blockind[h, h * N:(h + 1) * N] = 1.0
    dmask = np.ones((N, HID), np.float32)
    dmask[N // 2:, HID - 1] = 0.0
    return {
        "c_ident": np.eye(N, dtype=np.float32),
        "c_identb": np.eye(N, dtype=np.float32).astype(bf),
        "c_sel": sel.astype(bf),
        "c_blockind": blockind,
        "c_nhot": np.tile(nhot, 2).astype(np.float32).reshape(N, 1),
        "c_dmask": dmask,
        "c_fold": np.tile(np.eye(HID, dtype=np.float32), (2, 2)),
    }


def pipelined(eng, stage_a, stage_b, n):
    stage_a(0, 0)
    with eng.Fori(0, n // 2 - 1) as t:
        for u in (0, 1):
            stage_a(2 * t + (u + 1), 1 - u)
            stage_b(2 * t + u, u)
    stage_a(n - 1, 1)
    stage_b(n - 2, 0)
    stage_b(n - 1, 1)


class Parts:
    pass


def build(nc, a, out):
    with ExitStack() as ctx:
        k = Parts()
        k.a = a
        k.sb = lambda c, name, shape, dt: c.enter_context(nc.sbuf_tensor(name, shape, dt))
        k.ps = lambda c, name, shape, dt=F32: c.enter_context(nc.psum_tensor(name, shape, dt))
        k.sem = lambda name: ctx.enter_context(nc.semaphore(name))
        sb = lambda name, shape, dt=F32: k.sb(ctx, name, shape, dt)
        k.x = sb("x_all", [N, B * C])
        k.negm = sb("negm", [N, B * N], BF16)
        k.ident = sb("ident", [N, N])
        k.identb = sb("identb", [N, N], BF16)
        k.stats = sb("ln_stats", [N, B, 6])
        k.nmean = sb("ln_negmean", [N, B])
        k.rstd = sb("ln_rstd", [N, B])
        k.nmT = sb("nodemask_cols", [N, B])
        k.w0 = sb("w0", [C, C])
        k.wsrc = sb("wa_src_bc", [C, N])
        k.wdst = sb("wa_dst_bc", [C, N])
        k.b0 = sb("b0_bc", [N, C])
        k.c0 = sb("b0_dot_a", [N, 1])
        k.w1T = sb("l1_w1T", [C, C])
        k.w2T = sb("l1_w2T", [C, C])
        k.b1 = sb("l1_b1", [C, 1])
        k.b2 = sb("l1_b2", [C, 1])
        k.wuT = sb("l1_wuT", [C, 2, C])
        k.bu = sb("l1_bu_bc", [N, C])
        k.wl2 = sb("l2_w", [C, C])
        k.wa = sb("l2_wa", [C, 2, HEADS])
        k.ab = sb("l2_ab", [HEADS, 1])
        k.p1T = sb("l3_w1T", [C, HID])
        k.pcol = sb("l3_cols", [N, 8])
        k.wgT = sb("l3_wgT", [C, C])
        k.wtT = sb("l3_wtT", [C, 2, C])
        k.bt = sb("l3_bt_bc", [N, C])
        with ExitStack() as mask_ctx:
            k.mask1 = k.sb(mask_ctx, "mask1", [N, B * N], BF16)
            phase_weights(nc, k, a)
            phase_load(nc, k, a)
            phase_gat(nc, k)
            phase_maxpass(nc, k)
        phase_heads(nc, k)
        phase_pairs(nc, k, a, out)


def phase_weights(nc, k, a):
    with ExitStack() as ctx:
        raw = k.sb(ctx, "w_raw", [N, 10, N], F32)
        acol = k.sb(ctx, "a_cols", [C, 2], F32)
        b0col = k.sb(ctx, "b0_col", [C, 1], F32)
        b0mat = k.sb(ctx, "b0_mat", [C, N], F32)
        ones = k.sb(ctx, "w_ones", [N, N], F32)
        w0T = k.sb(ctx, "w0T", [C, C], F32)
        l2wT = k.sb(ctx, "l2_wT", [C, C], F32)
        aT = k.sb(ctx, "l2_aT", [C, 2, HEADS], F32)
        wacol = k.sb(ctx, "wa_cols", [C, 2], F32)
        ps = k.ps(ctx, "w_ps", [N, 8, 512])
        loaded, turned, copied, folded, spread = (k.sem(n) for n in (
            "w_loaded", "w_turned", "w_copied", "w_folded", "w_spread"))
        n_load = [0]
        turns = [
            (a["L0_gnn_W"], N, w0T[:, :]), (a["L1_gnn_W1"], N, k.w1T[:, :]), (a["L1_gnn_W2"], N, k.w2T[:, :]),
            (a["L1_gnn_Wu"][:, 0:C], N, k.wuT[:, 0, :]), (a["L1_gnn_Wu"][:, C:2 * C], N, k.wuT[:, 1, :]),
            (a["L2_gnn_W"], N, l2wT[:, :]), (a["L3_gnn_W1"], HID, k.p1T[:, :]), (a["L3_gnn_Wg"], N, k.wgT[:, :]),
            (a["L3_gnn_Wt"][:, 0:C], N, k.wtT[:, 0, :]), (a["L3_gnn_Wt"][:, C:2 * C], N, k.wtT[:, 1, :]),
        ]
        a2raw = k.sb(ctx, "l2_a_raw", [HEADS, 2 * C], F32)
        nmraw = k.sb(ctx, "nodemask_raw", [B, N], F32)
        col = lambda v, n: v.rearrange("(p o) -> p o", o=1)[0:n]
        row = lambda v, n: v.rearrange("(o c) -> o c", o=1).broadcast_to([n, v.shape[0]])
        with nc.Block() as block:
            @block.sync
            def _(sp):
                def load(dst, src):
                    sp.dma_start(dst, src).then_inc(loaded, 16)
                    n_load[0] += 1
                load(k.ident[:, :], a["c_ident"])
                load(k.identb[:, :], a["c_identb"])
                for i, (src, rows, _) in enumerate(turns):
                    load(raw[0:rows, i, :], src)
                load(a2raw[:, :], a["L2_gnn_a_w"])
                load(nmraw[:, :], a["nodemask"])
                load(k.w0[:, :], a["L0_gnn_W"])
                load(k.wl2[:, :], a["L2_gnn_W"])
                load(acol[:, 0:1], col(a["L0_gnn_a"][0:C], C))
                load(acol[:, 1:2], col(a["L0_gnn_a"][C:2 * C], C))
                load(b0col[:, :], col(a["L0_gnn_b"], C))
                load(k.b1[:, :], col(a["L1_gnn_b1"], C))
                load(k.b2[:, :], col(a["L1_gnn_b2"], C))
                load(k.ab[:, :], col(a["L2_gnn_a_b"], HEADS))
                load(k.b0[:, :], row(a["L0_gnn_b"], N))
                load(k.bu[:, :], row(a["L1_gnn_bu"], N))
                load(k.bt[:, :], row(a["L3_gnn_bt"], N))
                for half in (0, HID):
                    rows = slice(half, half + HID)
                    load(k.pcol[rows, 0:1], col(a["L3_gnn_b1"], HID))
                    load(k.pcol[rows, 1:2], col(a["L3_gnn_g1"], HID))
                    load(k.pcol[rows, 2:3], col(a["L3_gnn_be1"], HID))
                    load(k.pcol[rows, 3:4], a["L3_gnn_W2"].rearrange("o c -> c o"))
                load(k.pcol[:, 4:5], a["L3_gnn_b2"].rearrange("(o c) -> o c", o=1).broadcast_to([N, 1]))
                load(k.pcol[:, 5:6], col(a["L3_gnn_bg"], C))
                load(k.pcol[:, 6:7], col(a["L3_gnn_gg"], C))
                load(k.pcol[:, 7:8], col(a["L3_gnn_beg"], C))
                sp.wait_ge(loaded, 16 * n_load[0])

            @block.tensor
            def _(pe):
                pe.wait_ge(loaded, 16 * n_load[0])
                for i, (_, rows, _) in enumerate(turns):
                    last = nc.tensor.transpose(ps[:, i // 4, (i % 4) * N:(i % 4) * N + rows], raw[0:rows, i, :],
                                               k.ident[0:rows, 0:rows])
                for s in (0, 1):
                    nc.tensor.transpose(ps[:, 3, s * HEADS:(s + 1) * HEADS], a2raw[:, s * C:(s + 1) * C],
                                        k.ident[0:HEADS, 0:HEADS])
                nc.tensor.transpose(ps[:, 3, N:N + B], nmraw[:, :], k.ident[0:B, 0:B]).then_inc(turned, 1)
                pe.wait_ge(copied, 1)
                nc.tensor.matmul(ps[:, 4, 0:2], w0T[:, :], acol[:, :], start=True, stop=True)
                nc.tensor.matmul(ps[:, 5, 0:2 * HEADS], l2wT[:, :], aT[:].rearrange("c s h -> c (s h)"), start=True, stop=True)
                nc.tensor.matmul(ps[:, 6, 0:2], b0mat[:, :], acol[:, :], start=True, stop=True).then_inc(folded, 1)

            @block.vector
            def _(dve):
                dve.wait_ge(loaded, 16 * n_load[0])
                nc.vector.memset(ones[:, :], 1.0).then_inc(spread, 1)
                dve.wait_ge(spread, 1)
                nc.vector.tensor_scalar(b0mat[:, :], ones[:, :], b0col[:, 0:1], None, ALU.mult)
                dve.wait_ge(turned, 1)
                for i, (_, rows, dst) in enumerate(turns):
                    nc.vector.tensor_copy(dst, ps[:, i // 4, (i % 4) * N:(i % 4) * N + rows])
                nc.vector.tensor_copy(aT[:].rearrange("c s h -> c (s h)"), ps[:, 3, 0:2 * HEADS])
                nc.vector.tensor_copy(k.nmT[:, :], ps[:, 3, N:N + B]).then_inc(copied, 1)
                dve.wait_ge(folded, 1)
                nc.vector.tensor_copy(wacol[:, :], ps[:, 4, 0:2])
                nc.vector.tensor_copy(k.wa[:].rearrange("c s h -> c (s h)"), ps[:, 5, 0:2 * HEADS])
                nc.vector.tensor_reduce(k.c0[:, :], ps[:, 6, 0:2], AX.X, ALU.add).then_inc(spread, 1)
                dve.wait_ge(spread, 2)
                nc.vector.tensor_scalar(k.wsrc[:, :], ones[:, :], wacol[:, 0:1], None, ALU.mult)
                nc.vector.tensor_scalar(k.wdst[:, :], ones[:, :], wacol[:, 1:2], None, ALU.mult)


def ln_stats(nc, k, g):
    for i in range(G):
        nc.vector.bn_stats(k.stats[:, bass.ds(g * G + i, 1), :], k.x[:, bass.ds((g * G + i) * C, C)])


def phase_norm(nc, k, tag):
    with ExitStack() as ctx:
        sb = lambda name: k.sb(ctx, f"{tag}_{name}", [N, B], F32)
        msum, mdif, squares, within, apart, ve, sd = (sb(n) for n in (
            "mean_sum", "mean_dif", "squares", "within", "apart", "var_eps", "std"))
        halves, parts, eps_added, rooted = (k.sem(f"{tag}_{n}") for n in ("halves", "parts", "eps_added", "rooted"))
        with nc.Block() as block:
            @block.vector
            def _(dve):
                mean = (k.stats[:, :, 1], k.stats[:, :, 4])
                summed = (k.stats[:, :, 2], k.stats[:, :, 5])
                nc.vector.tensor_tensor(msum[:, :], mean[0], mean[1], ALU.add)
                nc.vector.tensor_tensor(mdif[:, :], mean[0], mean[1], ALU.subtract)
                nc.vector.tensor_tensor(squares[:, :], summed[0], summed[1], ALU.add).then_inc(halves, 1)
                dve.wait_ge(halves, 1)
                nc.vector.tensor_scalar(k.nmean[:, :], msum[:, :], -0.5, None, ALU.mult)
                nc.vector.tensor_scalar(within[:, :], squares[:, :], 1.0 / C, EPS, ALU.mult, ALU.add)
                nc.vector.tensor_tensor(apart[:, :], mdif[:, :], mdif[:, :], ALU.mult).then_inc(parts, 1)
                dve.wait_ge(parts, 1)
                nc.vector.scalar_tensor_tensor(out=ve[:, :], in0=apart[:, :], scalar=0.25, in1=within[:, :],
                                               op0=ALU.mult, op1=ALU.add).then_inc(eps_added, 1)
                dve.wait_ge(rooted, 1)
                nc.vector.reciprocal(k.rstd[:, :], sd[:, :])

            @block.scalar
            def _(act):
                act.wait_ge(eps_added, 1)
                nc.scalar.activation(sd[:, :], ve[:, :], ACT.Sqrt).then_inc(rooted, 1)


def normalize(nc, k, pool, xn, g, centered, normed):
    rows = lambda v: v.rearrange("n (b c) -> n b c", c=C)
    per_row = lambda v: v[:, bass.ds(g * G, G)].unsqueeze(2).broadcast_to([N, G, C])
    nc.gpsimd.tensor_tensor(rows(xn), rows(k.x[:, bass.ds(g * QC, QC)]), per_row(k.nmean), ALU.add).then_inc(centered, 1)
    pool.wait_ge(centered, done(g))
    nc.gpsimd.tensor_tensor(rows(xn), rows(xn), per_row(k.rstd), ALU.mult).then_inc(normed, 1)


def phase_load(nc, k, a):
    with ExitStack() as ctx:
        ring = k.sb(ctx, "adj_ring", [N, 2, QC], I32)
        x_in, masked = (k.sem(n) for n in ("x_in", "masked"))
        adj_in = [k.sem("adj_in0"), k.sem("adj_in1")]
        with nc.Block() as block:
            @block.scalar
            def _(act):
                for g in range(QUADS):
                    if g >= 1:
                        act.wait_ge(x_in, 16 * g)
                    act.dma_start(k.x[:, g * QC:(g + 1) * QC].rearrange("n (b c) -> n b c", c=C),
                                  a["x"][g * G:(g + 1) * G].rearrange("b n c -> n b c")).then_inc(x_in, 16)

            @block.sync
            def _(sp):
                for g in range(QUADS):
                    if g >= 2:
                        sp.wait_ge(masked, g - 1)
                    sp.dma_start(ring[:, g % 2, :].rearrange("n (b c) -> n b c", c=N),
                                 a["adj"][g * G:(g + 1) * G].rearrange("b n m -> n b m")).then_inc(adj_in[g % 2], 16)

            @block.vector
            def _(dve):
                for g in range(QUADS):
                    cols = slice(g * QC, (g + 1) * QC)
                    dve.wait_ge(adj_in[g % 2], 16 * (g // 2 + 1))
                    nc.vector.tensor_scalar(k.negm[:, cols], ring[:, g % 2, :], 0, -BIG, ALU.is_le, ALU.mult)
                    nc.vector.tensor_scalar(k.mask1[:, cols], ring[:, g % 2, :], 0, None, ALU.not_equal).then_inc(masked, 1)
                    dve.wait_ge(x_in, 16 * (g + 1))
                    ln_stats(nc, k, g)


def phase_gat(nc, k):
    phase_norm(nc, k, "n0")
    with ExitStack() as ctx:
        sb = lambda name, shape, dt=F32: k.sb(ctx, "g_" + name, shape, dt)
        xn = sb("xn", [N, 2, QC])
        hT = sb("hT", [C, 2, QC])
        hs = sb("h", [N, 2, QC])
        el = sb("el", [N, 2, QC])
        ex = sb("ex", [N, 2, QC])
        exT = sb("exT", [N, 2, QC])
        nmx = sb("nmx", [N, 2, G])
        zs = sb("zs", [N, 2, G])
        rz = sb("rz", [N, 2, G])
        psT, psH, psE, psD, psO = (k.ps(ctx, "g_" + n, [N, QC]) for n in ("psT", "psH", "psE", "psD", "psO"))
        sem = lambda name: k.sem("g_" + name)
        centered, normed, transposed, relued, h_mm, h_ready, e_mm, e_copied, leaky, negmax, expd = (sem(n) for n in (
            "centered", "normed", "transposed", "relued", "h_mm", "h_ready", "e_mm", "e_copied", "leaky", "negmax", "expd"))
        ex_turned, exT_ready, recip, scaled, out_mm, added = (sem(n) for n in (
            "ex_turned", "exT_ready", "recip", "scaled", "out_mm", "added"))
        b = lambda i: slice(i * N, (i + 1) * N)
        with nc.Block() as block:
            @block.gpsimd
            def _(pool):
                for s in (centered, normed):
                    pool.sem_inc(s, BIAS)

                def step(g, p):
                    pool.wait_ge(transposed, done(g - 2))
                    normalize(nc, k, pool, xn[:, p, :], g, centered, normed)
                with pool.Fori(0, QUADS // 2) as t:
                    for u in (0, 1):
                        step(2 * t + u, u)

            @block.tensor
            def _(pe):
                for s in (transposed, h_mm, e_mm, ex_turned, out_mm):
                    pe.sem_inc(s, BIAS)

                def stage_a(g, p):
                    pe.wait_ge(normed, done(g))
                    pe.wait_ge(relued, done(g - 1))
                    for i in range(G):
                        last = nc.tensor.transpose(psT[:, b(i)], xn[:, p, b(i)], k.ident[:, :])
                    last.then_inc(transposed, 1)
                    pe.wait_ge(relued, done(g))
                    pe.wait_ge(h_ready, done(g - 1))
                    for i in range(G):
                        last = nc.tensor.matmul(psH[:, b(i)], hT[:, p, b(i)], k.w0[:, :], start=True, stop=True)
                    last.then_inc(h_mm, 1)
                    pe.wait_ge(e_copied, done(g - 1))
                    nc.tensor.matmul(psE[:, :], k.wdst[:, :], hT[:, p, :], start=True, stop=False)
                    nc.tensor.matmul(psE[:, :], k.identb[:, :], k.negm[:, bass.ds(g * QC, QC)], start=False, stop=False)
                    for i in range(G):
                        last = nc.tensor.matmul(psE[:, b(i)], hT[:, p, b(i)], k.wsrc[:, :], start=False, stop=i == G - 1)
                    last.then_inc(e_mm, 1)

                def stage_b(g, p):
                    pe.wait_ge(expd, done(g))
                    pe.wait_ge(exT_ready, done(g - 1))
                    for i in range(G):
                        last = nc.tensor.transpose(psD[:, b(i)], ex[:, p, b(i)], k.ident[:, :])
                    last.then_inc(ex_turned, 1)
                    pe.wait_ge(exT_ready, done(g))
                    pe.wait_ge(h_ready, done(g))
                    pe.wait_ge(added, done(g - 1))
                    for i in range(G):
                        last = nc.tensor.matmul(psO[:, b(i)], exT[:, p, b(i)], hs[:, p, b(i)], start=True, stop=True)
                    last.then_inc(out_mm, 1)
                pipelined(pe, stage_a, stage_b, QUADS)

            @block.scalar
            def _(act):
                for s in (relued, e_copied, expd):
                    act.sem_inc(s, BIAS)

                def stage_a(g, p):
                    act.wait_ge(transposed, done(g))
                    act.wait_ge(e_mm, done(g - 2))
                    nc.scalar.activation(hT[:, p, :], psT[:, :], ACT.Relu).then_inc(relued, 1)
                    act.wait_ge(e_mm, done(g))
                    act.wait_ge(expd, done(g - 2))
                    nc.scalar.activation(el[:, p, :], psE[:, :], ACT.Identity, bias=k.c0[:, 0:1]).then_inc(e_copied, 1)

                def stage_b(g, p):
                    act.wait_ge(negmax, done(g))
                    act.wait_ge(ex_turned, done(g - 2))
                    act.wait_ge(recip, done(g - 2))
                    for i in range(G):
                        last = nc.scalar.activation(ex[:, p, b(i)], el[:, p, b(i)], ACT.Exp, bias=nmx[:, p, i:i + 1],
                                                    accum_out=zs[:, p, i:i + 1])
                    last.then_inc(expd, 1)
                pipelined(act, stage_a, stage_b, QUADS)

            @block.vector
            def _(dve):
                for s in (h_ready, leaky, negmax, exT_ready, recip, scaled, added):
                    dve.sem_inc(s, BIAS)

                def stage_a(g, p):
                    dve.wait_ge(h_mm, done(g))
                    dve.wait_ge(out_mm, done(g - 2))
                    nc.vector.tensor_tensor(
                        hs[:, p, :].rearrange("n (b c) -> n b c", c=C), psH[:, :].rearrange("n (b c) -> n b c", c=C),
                        k.b0[:, :].unsqueeze(1).broadcast_to([N, G, C]), ALU.add).then_inc(h_ready, 1)
                    dve.wait_ge(e_copied, done(g))
                    nc.vector.scalar_tensor_tensor(out=el[:, p, :], in0=el[:, p, :], scalar=0.01, in1=el[:, p, :],
                                                   op0=ALU.mult, op1=ALU.max).then_inc(leaky, 1)
                    dve.wait_ge(leaky, done(g))
                    dve.wait_ge(expd, done(g - 2))
                    nc.vector.tensor_reduce(nmx[:, p, :], el[:, p, :].rearrange("n (b c) -> n b c", c=N), AX.X, ALU.max,
                                            negate=True).then_inc(negmax, 1)

                def stage_b(g, p):
                    dve.wait_ge(ex_turned, done(g))
                    dve.wait_ge(out_mm, done(g - 2))
                    nc.vector.tensor_copy(exT[:, p, :], psD[:, :]).then_inc(exT_ready, 1)
                    dve.wait_ge(expd, done(g))
                    dve.wait_ge(scaled, done(g - 1))
                    nc.vector.reciprocal(rz[:, 0, :], zs[:, p, :]).then_inc(recip, 1)
                    dve.wait_ge(recip, done(g))
                    nc.vector.tensor_tensor(rz[:, 1, :], rz[:, 0, :], k.nmT[:, bass.ds(g * G, G)], ALU.mult).then_inc(scaled, 1)
                    dve.wait_ge(scaled, done(g))
                    dve.wait_ge(out_mm, done(g))
                    for i in range(G):
                        xs = k.x[:, bass.ds((g * G + i) * C, C)]
                        last = nc.vector.scalar_tensor_tensor(out=xs, in0=psO[:, b(i)], scalar=rz[:, 1, i:i + 1], in1=xs,
                                                              op0=ALU.mult, op1=ALU.add)
                    last.then_inc(added, 1)
                    dve.wait_ge(added, done(g))
                    ln_stats(nc, k, g)
                pipelined(dve, stage_a, stage_b, QUADS)


def phase_maxpass(nc, k):
    phase_norm(nc, k, "n1")
    with ExitStack() as ctx:
        sb = lambda name, shape, dt=F32: k.sb(ctx, "m_" + name, shape, dt)
        PADN = NBLK * BLK
        xn = sb("xn", [N, 2, QC])
        hT = sb("hT", [C, 2, QC])
        m1 = sb("m1", [C, 2, QC])
        m2 = sb("m2", [C, 2, G, PADN])
        table = sb("table", [C, G, NBLK, SUB])
        tableT = sb("tableT", [N, 2, 4, C])
        onehot = sb("onehot", [N, 2, 4, N])
        part = sb("part", [C, G, NG, N])
        mx = sb("mx", [C, QC])
        mT = sb("mT", [C, 2, QC])
        upd = sb("upd", [N, QC])
        sel = sb("sel", [N, NCH * 128], BF16)
        nhot = sb("nhot", [N, 1])
        psF, psTT, psC, psU = (k.ps(ctx, "m_" + n, [N, QC]) for n in ("psF", "psTT", "psC", "psU"))
        psS = k.ps(ctx, "m_psS", [N, 4, 512])
        sem = lambda name: k.sem("m_" + name)
        consts, padded, centered, normed, transposed, relued, m2_mm, m2_copied, m1_mm, m1_copied = (sem(n) for n in (
            "consts", "padded", "centered", "normed", "transposed", "relued", "m2_mm", "m2_copied", "m1_mm", "m1_copied"))
        grown, tabled, t_turned, tT_ready, match_mm, onehot_ready = (sem(n) for n in (
            "grown", "tabled", "t_turned", "tT_ready", "match_mm", "onehot_ready"))
        selected, reduced, merged, summed, mT_ready, u_mm, biased, added = (sem(n) for n in (
            "selected", "reduced", "merged", "summed", "mT_ready", "u_mm", "biased", "added"))
        b = lambda i: slice(i * N, (i + 1) * N)
        with nc.Block() as block:
            @block.sync
            def _(sp):
                sp.dma_start(sel[:, :], k.a["c_sel"]).then_inc(consts, 16)
                sp.dma_start(nhot[:, :], k.a["c_nhot"]).then_inc(consts, 16)
                sp.wait_ge(consts, 32)

            @block.gpsimd
            def _(pool):
                for s in (centered, normed):
                    pool.sem_inc(s, BIAS)

                def step(g, p):
                    pool.wait_ge(transposed, done(g - 2))
                    normalize(nc, k, pool, xn[:, p, :], g, centered, normed)
                with pool.Fori(0, QUADS // 2) as t:
                    for u in (0, 1):
                        step(2 * t + u, u)

            @block.tensor
            def _(pe):
                for s in (transposed, m2_mm, m1_mm, t_turned, match_mm, selected, u_mm):
                    pe.sem_inc(s, BIAS)
                pe.wait_ge(consts, 32)

                def front(g, p):
                    pe.wait_ge(normed, done(g))
                    pe.wait_ge(m1_copied, done(g - 1))
                    for i in range(G):
                        last = nc.tensor.transpose(psF[:, b(i)], xn[:, p, b(i)], k.ident[:, :])
                    last.then_inc(transposed, 1)
                    pe.wait_ge(relued, done(g))
                    nc.tensor.matmul(psF[:, :], k.w2T[:, :], hT[:, p, :], start=True, stop=True).then_inc(m2_mm, 1)
                    pe.wait_ge(m2_copied, done(g))
                    nc.tensor.matmul(psF[:, :], k.w1T[:, :], hT[:, p, :], start=True, stop=True).then_inc(m1_mm, 1)

                def prepare(g, i, r):
                    n = (g * G + i) * NG + r
                    chunks = range(4 * r, min(4 * r + 4, NCH))
                    pe.wait_ge(tT_ready, done(n - 1))
                    for c in chunks:
                        last = nc.tensor.transpose(psTT[:, b(c % 4)],
                                                   table[:, i, 2 * c:2 * c + 2, :].rearrange("z q s -> z (q s)"), k.ident[:, :])
                    last.then_inc(t_turned, 1)
                    pe.wait_ge(onehot_ready, done(n - 1))
                    for c in chunks:
                        last = nc.tensor.matmul(psC[:, b(c % 4)], sel[:, c * 128:(c + 1) * 128],
                                                k.mask1[:, bass.ds((g * G + i) * N, N)], start=True, stop=True)
                    last.then_inc(match_mm, 1)

                def select(g, i, r):
                    n = (g * G + i) * NG + r
                    par = (i * NG + r) % 2
                    pe.wait_ge(tT_ready, done(n))
                    pe.wait_ge(onehot_ready, done(n))
                    pe.wait_ge(reduced, done(n - 2))
                    for c in range(4 * r, min(4 * r + 4, NCH)):
                        for q in (0, 1):
                            rows = slice(SUB * q, SUB * q + SUB)
                            last = nc.tensor.matmul(psS[:, 2 * par + q, b(c % 4)], tableT[rows, par, c % 4, :],
                                                    onehot[rows, par, c % 4, :], start=True, stop=True)
                    last.then_inc(selected, 1)

                def back(g, p):
                    pe.wait_ge(tabled, done(g))
                    items = [(i, r) for i in range(G) for r in range(NG)]
                    prepare(g, *items[0])
                    for at, item in enumerate(items):
                        if at + 1 < len(items):
                            prepare(g, *items[at + 1])
                        select(g, *item)
                    pe.wait_ge(mT_ready, done(g))
                    pe.wait_ge(biased, done(g - 1))
                    for i in range(G):
                        nc.tensor.matmul(psU[:, b(i)], hT[:, p, b(i)], k.wuT[:, 0, :], start=True, stop=False)
                        last = nc.tensor.matmul(psU[:, b(i)], mT[:, p, b(i)], k.wuT[:, 1, :], start=False, stop=True)
                    last.then_inc(u_mm, 1)
                pipelined(pe, front, back, QUADS)

            @block.scalar
            def _(act):
                for s in (relued, m2_copied, m1_copied, tT_ready, onehot_ready, mT_ready):
                    act.sem_inc(s, BIAS)
                act.wait_ge(consts, 32)

                def front(g, p):
                    act.wait_ge(transposed, done(g))
                    act.wait_ge(u_mm, done(g - 2))
                    nc.scalar.activation(hT[:, p, :], psF[:, :], ACT.Relu).then_inc(relued, 1)
                    act.wait_ge(m2_mm, done(g))
                    act.wait_ge(tabled, done(g - 2))
                    act.wait_ge(padded, 1)
                    nc.scalar.activation(m2[:, p, :, 0:N], psF[:, :].rearrange("z (b n) -> z b n", n=N), ACT.Identity,
                                         bias=k.b2[:, 0:1]).then_inc(m2_copied, 1)
                    act.wait_ge(m1_mm, done(g))
                    act.wait_ge(summed, done(g - 2))
                    nc.scalar.activation(m1[:, p, :], psF[:, :], ACT.Identity, bias=k.b1[:, 0:1]).then_inc(m1_copied, 1)

                def back(g, p):
                    for i in range(G):
                        for r in range(NG):
                            n = (g * G + i) * NG + r
                            w = min(4, NCH - 4 * r) * N
                            flat = lambda t: t[:, (i * NG + r) % 2, :, :].rearrange("r c n -> r (c n)")[:, 0:w]
                            act.wait_ge(t_turned, done(n))
                            act.wait_ge(selected, done(n - 2))
                            nc.scalar.activation(flat(tableT), psTT[:, 0:w], ACT.Copy).then_inc(tT_ready, 1)
                            act.wait_ge(match_mm, done(n))
                            nc.scalar.activation(flat(onehot), psC[:, 0:w], ACT.Relu, bias=nhot[:, 0:1]).then_inc(onehot_ready, 1)
                    act.wait_ge(summed, done(g))
                    nc.scalar.activation(mT[:, p, :], mx[:, :], ACT.Relu).then_inc(mT_ready, 1)
                pipelined(act, front, back, QUADS)

            @block.vector
            def _(dve):
                for s in (tabled, reduced, merged, summed, biased, added):
                    dve.sem_inc(s, BIAS)
                nc.vector.memset(table[:].rearrange("z b k s -> z (b k s)"), 0.0).then_inc(padded, 1)
                dve.wait_ge(padded, 1)
                nc.vector.memset(table[:, :, 0:NBLK, 0], LOWEST)
                nc.vector.memset(m2[:, :, :, N:PADN].rearrange("z p b j -> z (p b) j"), LOWEST).then_inc(padded, 1)
                dve.wait_ge(padded, 2)

                def tables(g, p):
                    dve.wait_ge(m2_copied, done(g))
                    dve.wait_ge(t_turned, done(G * NG * g - 1))
                    for i in range(G):
                        node = m2[:, p, i, :].rearrange("z (k t) -> z k t", t=BLK)
                        for t in range(BLK):
                            w = 2 ** t
                            last = nc.vector.tensor_tensor(table[:, i, 0:NBLK, w:2 * w], table[:, i, 0:NBLK, 0:w],
                                                           node[:, :, t:t + 1].broadcast_to([C, NBLK, w]), ALU.max)
                            last.then_inc(grown if t < BLK - 1 or i < G - 1 else tabled, 1)
                            if t < BLK - 1:
                                dve.wait_ge(grown, g * (G * BLK - 1) + i * BLK + t + 1)

                def rounds(g, p):
                    for i in range(G):
                        for r in range(NG):
                            n = (g * G + i) * NG + r
                            par = (i * NG + r) % 2
                            w = min(4, NCH - 4 * r) * N
                            dve.wait_ge(selected, done(n))
                            dve.wait_ge(merged, done(g - 1))
                            nc.vector.tensor_reduce(
                                part[:, i, r, :],
                                psS[:, 2 * par:2 * par + 2, 0:w].rearrange("z q (c i) -> z i q c", i=N),
                                AX.XY, ALU.max).then_inc(reduced, 1)
                    dve.wait_ge(reduced, done(G * NG * g + G * NG - 1))
                    dve.wait_ge(mT_ready, done(g - 1))
                    nc.vector.tensor_reduce(mx[:].rearrange("z (b i) -> z b i", i=N), part[:].rearrange("z b r i -> z b i r"),
                                            AX.X, ALU.max).then_inc(merged, 1)
                    dve.wait_ge(merged, done(g))
                    nc.vector.tensor_tensor(mx[:, :], mx[:, :], m1[:, p, :], ALU.add).then_inc(summed, 1)

                def update(g, p):
                    dve.wait_ge(u_mm, done(g))
                    dve.wait_ge(added, done(g - 1))
                    nc.vector.tensor_tensor(
                        upd[:, :].rearrange("n (b c) -> n b c", c=C), psU[:, :].rearrange("n (b c) -> n b c", c=C),
                        k.bu[:, :].unsqueeze(1).broadcast_to([N, G, C]), ALU.add).then_inc(biased, 1)
                    dve.wait_ge(biased, done(g))
                    xs = k.x[:, bass.ds(g * QC, QC)]
                    nc.vector.scalar_tensor_tensor(out=xs, in0=upd[:, :], scalar=0.0, in1=xs, op0=ALU.max,
                                                   op1=ALU.add).then_inc(added, 1)
                    dve.wait_ge(added, done(g))
                    ln_stats(nc, k, g)

                tables(0, 0)
                with dve.Fori(0, QUADS // 2 - 1) as t:
                    for u in (0, 1):
                        rounds(2 * t + u, u)
                        tables(2 * t + (u + 1), 1 - u)
                        update(2 * t + u, u)
                rounds(QUADS - 2, 0)
                tables(QUADS - 1, 1)
                update(QUADS - 2, 0)
                rounds(QUADS - 1, 1)
                update(QUADS - 1, 1)


def phase_heads(nc, k):
    phase_norm(nc, k, "n2")
    with ExitStack() as ctx:
        sb = lambda name, shape, dt=F32: k.sb(ctx, "a_" + name, shape, dt)
        HC = HEADS * N
        KR = 32 + HEADS
        xn = sb("xn", [N, 2, QC])
        hT = sb("hT", [C, QC])
        hs = sb("h", [N, 2, QC])
        lhs = sb("lhs", [KR, 2, QC])
        s2 = sb("s2", [KR, 2, QC])
        ind = sb("ind", [KR, HC])
        rhs = sb("rhs", [KR, 2, HC])
        eu = sb("eu", [N, 2, HC])
        ex = sb("ex", [N, 2, HC])
        nmx = sb("nmx", [N, 2, HEADS])
        zs = sb("zs", [N, 2, HEADS])
        rz = sb("rz", [N, 2, HEADS])
        diag = sb("diag", [N, 2, HC])
        attT = sb("attT", [N, 2, N])
        psF, psA, psO = (k.ps(ctx, "a_" + n, [N, QC]) for n in ("psF", "psA", "psO"))
        psE = k.ps(ctx, "a_psE", [N, 2, HC])
        sem = lambda name: k.sem("a_" + name)
        consts, cleared, centered, normed, transposed, relued, h_mm, h_ready, s_mm, s_ready = (sem(n) for n in (
            "consts", "cleared", "centered", "normed", "transposed", "relued", "h_mm", "h_ready", "s_mm", "s_ready"))
        placed, e_mm, e_copied, leaky, negmax, expd = (sem(n) for n in (
            "placed", "e_mm", "e_copied", "leaky", "negmax", "expd"))
        recip, diag_ready, att_mm, att_ready, out_mm, added = (sem(n) for n in (
            "recip", "diag_ready", "att_mm", "att_ready", "out_mm", "added"))
        b = lambda i: slice(i * N, (i + 1) * N)

        def quads(eng, prologue, iteration):
            prologue()
            with eng.Fori(0, QUADS // 2 - 1) as t:
                for u in (0, 1):
                    iteration(2 * t + u, u, True)
            iteration(QUADS - 2, 0, True)
            iteration(QUADS - 1, 1, False)

        with nc.Block() as block:
            @block.sync
            def _(sp):
                sp.wait_ge(cleared, 1)
                sp.dma_start(ind[32:KR, :], k.a["c_blockind"]).then_inc(consts, 16)
                for p in (0, 1):
                    sp.dma_start(rhs[0:HEADS, p, :], k.a["c_blockind"]).then_inc(consts, 16)
                sp.wait_ge(consts, 48)

            @block.gpsimd
            def _(pool):
                for s in (centered, normed, placed):
                    pool.sem_inc(s, BIAS)
                pool.wait_ge(consts, 48)

                def norm(g, p):
                    pool.wait_ge(transposed, done(g - 2))
                    normalize(nc, k, pool, xn[:, p, :], g, centered, normed)

                def iteration(g, p, with_next):
                    if with_next:
                        pool.wait_ge(placed, done(g * G - 1))
                        norm(g + 1, 1 - p)
                        pool.wait_ge(normed, done(g + 1))
                    pool.wait_ge(s_ready, done(g))
                    for i in range(G):
                        pool.wait_ge(e_mm, done(g * G + (i - 2)))
                        nc.gpsimd.tensor_tensor(
                            rhs[32:KR, i % 2, :].rearrange("r (h j) -> r h j", j=N), ind[32:KR, :].rearrange("r (h j) -> r h j", j=N),
                            s2[32:KR, p, b(i)].unsqueeze(1).broadcast_to([HEADS, HEADS, N]), ALU.mult).then_inc(placed, 1)
                quads(pool, lambda: norm(0, 0), iteration)

            @block.tensor
            def _(pe):
                for s in (transposed, h_mm, s_mm, e_mm, att_mm, out_mm):
                    pe.sem_inc(s, BIAS)
                pe.wait_ge(consts, 48)

                def front(g, p):
                    pe.wait_ge(normed, done(g))
                    pe.wait_ge(s_ready, done(g - 1))
                    for i in range(G):
                        last = nc.tensor.transpose(psF[:, b(i)], xn[:, p, b(i)], k.ident[:, :])
                    last.then_inc(transposed, 1)
                    pe.wait_ge(relued, done(g))
                    for i in range(G):
                        last = nc.tensor.matmul(psF[:, b(i)], hT[:, b(i)], k.wl2[:, :], start=True, stop=True)
                    last.then_inc(h_mm, 1)
                    pe.wait_ge(h_ready, done(g))
                    nc.tensor.matmul(psF[0:HEADS, :], k.wa[:, 0, :], hT[:, :], start=True, stop=True)
                    nc.tensor.matmul(psF[32:KR, :], k.wa[:, 1, :], hT[:, :], start=True, stop=True).then_inc(s_mm, 1)

                def scores(g, p, i):
                    n = g * G + i
                    pe.wait_ge(s_ready, done(g))
                    pe.wait_ge(placed, done(n))
                    pe.wait_ge(e_copied, done(n - 2))
                    for half in (0, 1):
                        at = psE[:, i % 2, half * 512:(half + 1) * 512]
                        nc.tensor.matmul(at, lhs[:, p, b(i)], rhs[:, i % 2, half * 512:(half + 1) * 512], start=True, stop=False)
                        last = nc.tensor.matmul(at.rearrange("n (h j) -> n h j", j=N), k.identb[:, :],
                                                k.negm[:, bass.ds(n * N, N)].unsqueeze(1).broadcast_to([N, 4, N]),
                                                start=False, stop=True)
                    last.then_inc(e_mm, 1)

                def attend(g, p, i):
                    n = g * G + i
                    pe.wait_ge(expd, done(n))
                    pe.wait_ge(diag_ready, done(n))
                    pe.wait_ge(att_ready, done(n - 1))
                    for h in range(HEADS):
                        last = nc.tensor.matmul(psA[:, 0:N], ex[:, i % 2, b(h)], diag[:, i % 2, b(h)],
                                                start=h == 0, stop=h == HEADS - 1)
                    last.then_inc(att_mm, 1)
                    pe.wait_ge(att_ready, done(n))
                    if i == 0:
                        pe.wait_ge(added, done(g - 1))
                    nc.tensor.matmul(psO[:, b(i)], attT[:, i % 2, :], hs[:, p, b(i)], start=True, stop=True).then_inc(out_mm, 1)

                def prologue():
                    front(0, 0)
                    scores(0, 0, 0)

                def iteration(g, p, with_next):
                    if with_next:
                        front(g + 1, 1 - p)
                    for i in range(G):
                        if i + 1 < G:
                            scores(g, p, i + 1)
                        elif with_next:
                            scores(g + 1, 1 - p, 0)
                        attend(g, p, i)
                quads(pe, prologue, iteration)

            @block.scalar
            def _(act):
                for s in (relued, e_copied, expd):
                    act.sem_inc(s, BIAS)

                def front(g, p):
                    act.wait_ge(transposed, done(g))
                    act.wait_ge(s_mm, done(g - 1))
                    nc.scalar.activation(hT[:, :], psF[:, :], ACT.Relu).then_inc(relued, 1)

                def scores(g, p, i):
                    n = g * G + i
                    act.wait_ge(e_mm, done(n))
                    act.wait_ge(expd, done(n - 2))
                    nc.scalar.activation(eu[:, i % 2, :], psE[:, i % 2, :], ACT.Copy).then_inc(e_copied, 1)

                def exps(g, p, i):
                    n = g * G + i
                    act.wait_ge(negmax, done(n))
                    act.wait_ge(att_mm, done(n - 2))
                    act.wait_ge(recip, done(n - 2))
                    for h in range(HEADS):
                        last = nc.scalar.activation(ex[:, i % 2, b(h)], eu[:, i % 2, b(h)], ACT.Exp,
                                                    bias=nmx[:, i % 2, h:h + 1], accum_out=zs[:, i % 2, h:h + 1])
                    last.then_inc(expd, 1)

                def prologue():
                    front(0, 0)
                    scores(0, 0, 0)

                def iteration(g, p, with_next):
                    if with_next:
                        front(g + 1, 1 - p)
                    for i in range(G):
                        if i + 1 < G:
                            scores(g, p, i + 1)
                        elif with_next:
                            scores(g + 1, 1 - p, 0)
                        exps(g, p, i)
                quads(act, prologue, iteration)

            @block.vector
            def _(dve):
                for s in (h_ready, s_ready, leaky, negmax, recip, diag_ready, att_ready, added):
                    dve.sem_inc(s, BIAS)
                nc.vector.memset(lhs[:].rearrange("r p c -> r (p c)"), 0.0)
                nc.vector.memset(rhs[:].rearrange("r p c -> r (p c)"), 0.0).then_inc(cleared, 1)
                dve.wait_ge(cleared, 1)
                nc.vector.memset(lhs[32:KR, :, :].rearrange("r p c -> r (p c)"), 1.0)

                def front(g, p):
                    dve.wait_ge(h_mm, done(g))
                    dve.wait_ge(out_mm, done(G * g - (G + 1)))
                    nc.vector.tensor_copy(hs[:, p, :], psF[:, :]).then_inc(h_ready, 1)
                    dve.wait_ge(s_mm, done(g))
                    dve.wait_ge(e_mm, done(G * g - (G + 1)))
                    nc.vector.tensor_scalar(lhs[0:HEADS, p, :], psF[0:HEADS, :], k.ab[:, 0:1], None, ALU.add)
                    nc.vector.tensor_copy(s2[32:KR, p, :], psF[32:KR, :]).then_inc(s_ready, 1)

                def scores(g, p, i):
                    n = g * G + i
                    dve.wait_ge(e_copied, done(n))
                    nc.vector.scalar_tensor_tensor(out=eu[:, i % 2, :], in0=eu[:, i % 2, :], scalar=0.01, in1=eu[:, i % 2, :],
                                                   op0=ALU.mult, op1=ALU.max).then_inc(leaky, 1)
                    dve.wait_ge(leaky, done(n))
                    dve.wait_ge(expd, done(n - 2))
                    nc.vector.tensor_reduce(nmx[:, i % 2, :], eu[:, i % 2, :].rearrange("n (h j) -> n h j", j=N), AX.X, ALU.max,
                                            negate=True).then_inc(negmax, 1)

                def attend(g, p, i):
                    n = g * G + i
                    dve.wait_ge(expd, done(n))
                    dve.wait_ge(diag_ready, done(n - 2))
                    nc.vector.reciprocal(rz[:, i % 2, :], zs[:, i % 2, :]).then_inc(recip, 1)
                    dve.wait_ge(recip, done(n))
                    dve.wait_ge(att_mm, done(n - 2))
                    for h in range(HEADS):
                        last = nc.vector.tensor_scalar(diag[:, i % 2, b(h)], k.ident[:, :], rz[:, i % 2, h:h + 1], 1.0 / HEADS,
                                                       ALU.mult, ALU.mult)
                    last.then_inc(diag_ready, 1)
                    dve.wait_ge(att_mm, done(n))
                    dve.wait_ge(out_mm, done(n - 2))
                    nc.vector.tensor_copy(attT[:, i % 2, :], psA[:, 0:N]).then_inc(att_ready, 1)

                def finish(g):
                    dve.wait_ge(out_mm, done(g * G + (G - 1)))
                    xs = k.x[:, bass.ds(g * QC, QC)]
                    nc.vector.tensor_tensor(xs, psO[:, :], xs, ALU.add).then_inc(added, 1)
                    dve.wait_ge(added, done(g))
                    ln_stats(nc, k, g)

                def prologue():
                    front(0, 0)
                    scores(0, 0, 0)

                def iteration(g, p, with_next):
                    if with_next:
                        front(g + 1, 1 - p)
                    for i in range(G):
                        if i + 1 < G:
                            scores(g, p, i + 1)
                        elif with_next:
                            scores(g + 1, 1 - p, 0)
                        attend(g, p, i)
                    finish(g)
                quads(dve, prologue, iteration)


DUP = N + HID
SLABS = 4
DS = 8
HALF = DS * N
SC = 2 * HALF


def phase_pairs(nc, k, a, out):
    phase_norm(nc, k, "n3")
    with ExitStack() as ctx:
        hd = k.sb(ctx, "hd", [C, B * DUP], F32)
        hy = k.sb(ctx, "hy", [N, B * C], F32)
        alpha = k.sb(ctx, "p_alpha", [N, 1], F32)
        beta = k.sb(ctx, "p_beta", [N, 1], F32)
        diag0 = k.sb(ctx, "p_diag0", [N, 2 * N], F32)
        ystats = k.sb(ctx, "y_stats", [C, B, 6], F32)
        scratch = nc.dram_tensor("pair_scores", (2, N * 2 * N), F32).ap()
        phase_pair_inputs(nc, k, hd, hy)
        with ExitStack() as dctx:
            dif = k.sb(dctx, "p_dif", [C, 2, SC], F32)
            phase_pair_stats(nc, k, hd, dif, alpha, beta, diag0)
            phase_pair_scores(nc, k, hd, hy, dif, alpha, beta, diag0, scratch, ystats)
        phase_output(nc, k, hd, hy, ystats, out)


def phase_pair_inputs(nc, k, hd, hy):
    with ExitStack() as ctx:
        xn = k.sb(ctx, "i_xn", [N, 2, QC], F32)
        hT = k.sb(ctx, "i_hT", [C, 2, QC], F32)
        psT, psH = k.ps(ctx, "i_psT", [N, QC]), k.ps(ctx, "i_psH", [N, QC])
        sem = lambda name: k.sem("i_" + name)
        centered, normed, transposed, relued, copied, h_mm, h_ready = (sem(n) for n in (
            "centered", "normed", "transposed", "relued", "copied", "h_mm", "h_ready"))
        b = lambda i: slice(i * N, (i + 1) * N)

        def quads(eng, step):
            with eng.Fori(0, QUADS // 2) as t:
                for u in (0, 1):
                    step(2 * t + u, u)

        with nc.Block() as block:
            @block.gpsimd
            def _(pool):
                for s in (centered, normed):
                    pool.sem_inc(s, BIAS)

                def step(g, p):
                    pool.wait_ge(transposed, done(g - 2))
                    normalize(nc, k, pool, xn[:, p, :], g, centered, normed)
                quads(pool, step)

            @block.tensor
            def _(pe):
                for s in (transposed, h_mm):
                    pe.sem_inc(s, BIAS)

                def step(g, p):
                    pe.wait_ge(normed, done(g))
                    pe.wait_ge(relued, done(g - 1))
                    for i in range(G):
                        last = nc.tensor.transpose(psT[:, b(i)], xn[:, p, b(i)], k.ident[:, :])
                    last.then_inc(transposed, 1)
                    pe.wait_ge(relued, done(g))
                    pe.wait_ge(h_ready, done(g - 1))
                    for i in range(G):
                        last = nc.tensor.matmul(psH[:, b(i)], hT[:, p, b(i)], k.wgT[:, :], start=True, stop=True)
                    last.then_inc(h_mm, 1)
                quads(pe, step)

            @block.scalar
            def _(act):
                for s in (relued, h_ready):
                    act.sem_inc(s, BIAS)

                def step(g, p):
                    act.wait_ge(transposed, done(g))
                    act.wait_ge(h_mm, done(g - 2))
                    act.wait_ge(copied, done(g - 2))
                    nc.scalar.activation(hT[:, p, :], psT[:, :], ACT.Relu).then_inc(relued, 1)
                    act.wait_ge(h_mm, done(g))
                    nc.scalar.activation(hy[:, bass.ds(g * QC, QC)], psH[:, :], ACT.Copy).then_inc(h_ready, 1)
                quads(act, step)

            @block.vector
            def _(dve):
                dve.sem_inc(copied, BIAS)

                def step(g, p):
                    dve.wait_ge(relued, done(g))
                    src = hT[:, p, :].rearrange("c (b n) -> c b n", n=N)
                    dst = hd[:, bass.ds(g * (G * DUP), G * DUP)].rearrange("c (b n) -> c b n", n=DUP)
                    nc.vector.tensor_copy(dst[:, :, 0:N], src)
                    nc.vector.tensor_copy(dst[:, :, N:DUP], src[:, :, 0:HID]).then_inc(copied, 1)
                quads(dve, step)


def windows(hd, n, s):
    one = hd[:, bass.ds(n * DUP, N)]
    far = hd[:, bass.ds(n * DUP + (1 + DS * s), N)]
    part = list(one.ap)[0]
    return (bass.AP(one.tensor, one.offset, [part, [0, 2], [0, DS], [1, N]]),
            bass.AP(far.tensor, far.offset, [part, [HID // 2, 2], [1, DS], [1, N]]))


def phase_pair_stats(nc, k, hd, dif, alpha, beta, diag0):
    with ExitStack() as ctx:
        sb = lambda name, shape, dt=F32: k.sb(ctx, "v_" + name, shape, dt)
        D = sb("abs", [C, SLABS, SC])
        dsum = sb("dsum", [C, B * SLABS])
        hsq = sb("hsq", [N, B * SLABS])
        junk = sb("junk", [N, 2, HALF])
        dsumv = sb("dsumv", [C, B])
        tot = sb("tot", [N, 3])
        fold = sb("fold", [N, N])
        ones = sb("ones", [N, N])
        v = sb("v", [N, 12])
        psW = k.ps(ctx, "v_psW", [N, 3, HALF])
        psS = k.ps(ctx, "v_psS", [N, 512])
        sem = lambda name: k.sem("v_" + name)
        cleared, consts, sub_done, vabs_done, abs_done, w_mm, squared, totals, folded, algebra, rooted, own_mm = (sem(n) for n in (
            "cleared", "consts", "sub_done", "vabs_done", "abs_done", "w_mm", "squared", "totals", "folded", "algebra", "rooted", "own_mm"))
        PAIRS = float(B * N * N)

        VCOLS = 1536

        def graphs(eng, step):
            step(0, 0, True)
            with eng.Fori(0, (B - 1) // 3) as t:
                for u in range(3):
                    step(3 * t + (u + 1), SLABS * (u + 1) % 3, False)

        with nc.Block() as block:
            @block.sync
            def _(sp):
                sp.dma_start(fold[:, :], k.a["c_fold"]).then_inc(consts, 16)
                sp.wait_ge(consts, 16)

            @block.vector
            def _(dve):
                for s in (sub_done, vabs_done):
                    dve.sem_inc(s, BIAS)
                nc.vector.memset(D[:, SLABS - 1, SC - HID:SC], 0.0)
                nc.vector.memset(ones[:, :], 1.0).then_inc(cleared, 1)

                def step(n, buf0, first):
                    for s in range(SLABS):
                        m = n * SLABS + s
                        dve.wait_ge(abs_done, done(m - 2))
                        if s == 1:
                            dve.wait_ge(vabs_done, done(n - 1))
                        one, far = windows(hd, n, s)
                        nc.vector.tensor_tensor(dif[:, s % 2, :].rearrange("c (h d i) -> c h d i", h=2, i=N), one, far,
                                                ALU.subtract).then_inc(sub_done, 1)
                    dve.wait_ge(sub_done, done(m))
                    dve.wait_ge(w_mm, done(m - SLABS))
                    nc.vector.scalar_tensor_tensor(
                        out=D[:, SLABS - 1, 0:VCOLS], in0=dif[:, 1, 0:VCOLS], scalar=-1.0, in1=dif[:, 1, 0:VCOLS],
                        op0=ALU.mult, op1=ALU.max, accum_out=dsumv[:, bass.ds(n, 1)]).then_inc(vabs_done, 1)
                graphs(dve, step)

                dve.wait_ge(squared, done(B * SLABS - 1))
                dve.wait_ge(vabs_done, done(B - 1))
                nc.vector.tensor_reduce(tot[:, 0:1], dsum[:, :], AX.X, ALU.add)
                nc.vector.tensor_reduce(tot[:, 2:3], dsumv[:, :], AX.X, ALU.add)
                nc.vector.tensor_reduce(tot[:, 1:2], hsq[:, :], AX.X, ALU.add).then_inc(totals, 1)
                at = [0]

                def link(ins):
                    at[0] += 1
                    ins.then_inc(algebra, 1)
                    dve.wait_ge(algebra, at[0])
                c = lambda i: v[:, i:i + 1]
                b1, g1, be1, w2, b2 = (k.pcol[:, i:i + 1] for i in range(5))
                dve.wait_ge(folded, 1)
                link(nc.vector.tensor_scalar(c(0), psS[:, 0:1], 2.0 / PAIRS, None, ALU.mult))
                link(nc.vector.tensor_scalar(c(1), psS[:, 1:2], 2.0 / PAIRS, None, ALU.mult))
                link(nc.vector.tensor_tensor(c(2), c(0), c(0), ALU.mult))
                link(nc.vector.tensor_tensor(c(3), c(1), c(2), ALU.subtract))
                link(nc.vector.tensor_scalar(c(4), c(3), EPS, None, ALU.add))
                dve.wait_ge(rooted, 1)
                link(nc.vector.reciprocal(c(6), c(5)))
                link(nc.vector.tensor_tensor(alpha[:, :], c(6), g1, ALU.mult))
                link(nc.vector.tensor_tensor(c(7), c(0), b1, ALU.add))
                link(nc.vector.tensor_tensor(c(7), b1, c(7), ALU.subtract))
                link(nc.vector.scalar_tensor_tensor(out=beta[:, :], in0=c(7), scalar=alpha[:, 0:1], in1=be1,
                                                    op0=ALU.mult, op1=ALU.add))
                link(nc.vector.scalar_tensor_tensor(out=c(8), in0=beta[:, :], scalar=0.01, in1=beta[:, :],
                                                    op0=ALU.mult, op1=ALU.max))
                link(nc.vector.tensor_tensor(c(9), c(8), w2, ALU.mult))
                link(nc.vector.tensor_scalar(junk[:, 0, 0:N], ones[:, :], c(9), None, ALU.mult))
                dve.wait_ge(own_mm, 1)
                link(nc.vector.tensor_tensor(c(10), psS[:, 4:5], b2, ALU.add))
                link(nc.vector.memset(diag0[:, :], 0.0))
                link(nc.vector.tensor_scalar(diag0[:, 0:N], k.ident[:, :], c(10), 0.5, ALU.mult, ALU.mult))

            @block.scalar
            def _(act):
                for s in (abs_done, squared):
                    act.sem_inc(s, BIAS)
                act.wait_ge(cleared, 1)

                def absolute(n, s):
                    m = n * SLABS + s
                    cols = slice(VCOLS, SC - HID) if s == SLABS - 1 else slice(0, SC)
                    act.wait_ge(sub_done, done(m))
                    act.wait_ge(w_mm, done(m - SLABS))
                    nc.scalar.activation(D[:, s, cols], dif[:, s % 2, cols], ACT.Abs,
                                         accum_out=dsum[:, bass.ds(m, 1)]).then_inc(abs_done, 1)

                def square(m, s, buf):
                    act.wait_ge(w_mm, done(m))
                    act.wait_ge(squared, done(m - 2))
                    nc.scalar.activation(junk[:, s % 2, :], psW[:, buf, :], ACT.Square,
                                         accum_out=hsq[:, bass.ds(m, 1)]).then_inc(squared, 1)

                def step(n, buf0, first):
                    for s in range(SLABS):
                        absolute(n, s)
                        if s >= 2 or not first:
                            square(n * SLABS + (s - 2), s, (buf0 + s + 1) % 3)
                graphs(act, step)
                for s in (2, 3):
                    square((B - 1) * SLABS + s, s, ((B - 1) * SLABS + s) % 3)
                act.wait_ge(algebra, 5)
                nc.scalar.activation(v[:, 5:6], v[:, 4:5], ACT.Sqrt).then_inc(rooted, 1)

            @block.tensor
            def _(pe):
                pe.sem_inc(w_mm, BIAS)
                pe.wait_ge(consts, 16)
                pe.wait_ge(cleared, 1)

                def step(n, buf0, first):
                    for s in range(SLABS):
                        m = n * SLABS + s
                        buf = (buf0 + s) % 3
                        pe.wait_ge(abs_done, done(m))
                        if s == SLABS - 1:
                            pe.wait_ge(vabs_done, done(n))
                        pe.wait_ge(squared, done(m - 3))
                        last = pair_product(nc, k, psW[:, buf, :], D[:, s, :])
                        last.then_inc(w_mm, 1)
                graphs(pe, step)
                pe.wait_ge(totals, 1)
                for half in (0, HID):
                    for part in (0, 2):
                        nc.tensor.matmul(psS[half:half + HID, 0:1], k.p1T[:, :], tot[:, part:part + 1], start=part == 0,
                                         stop=part == 2)
                nc.tensor.matmul(psS[:, 1:2], fold[:, :], tot[:, 1:2], start=True, stop=True).then_inc(folded, 1)
                pe.wait_ge(algebra, 13)
                nc.tensor.matmul(psS[:, 4:5], junk[0:HID, 0, 0:N], ones[0:HID, 0:1], start=True, stop=True).then_inc(own_mm, 1)


def pair_product(nc, k, ps, D):
    for c in range(0, HALF, 512):
        nc.tensor.matmul(ps[0:HID, c:c + 512], k.p1T[:, :], D[:, c:c + 512], start=True, stop=True)
        last = nc.tensor.matmul(ps[HID:N, c:c + 512], k.p1T[:, :], D[:, HALF + c:HALF + c + 512], start=True, stop=True)
    return last


def phase_pair_scores(nc, k, hd, hy, dif, alpha, beta, diag0, scratch, ystats):
    with ExitStack() as ctx:
        sb = lambda name, shape, dt=F32: k.sb(ctx, "s_" + name, shape, dt)
        D = sb("abs", [C, 2, SC])
        place = sb("place", [N, 2, 32])
        dmask = sb("dmask", [N, HID])
        hid = sb("hid", [N, SLABS, HALF])
        rows = sb("rows", [N, 512])
        rot = sb("rot", [N, 2, HID])
        wide = sb("wide", [N, 2, 2 * N])
        fwd = sb("fwd", [N, 2, N])
        nmx = sb("nmx", [N, 2])
        zs = sb("zs", [N, 2])
        rz = sb("rz", [N, 2])
        ex = sb("ex", [N, 2, N])
        dg = sb("dg", [N, 2, N])
        attT = sb("attT", [N, 2, N])
        hg = sb("hg", [N, 2, C])
        psW = k.ps(ctx, "s_psW", [N, 2, HALF])
        psR, psT, psM, psA = (k.ps(ctx, "s_" + n, [N, 512]) for n in ("psR", "psT", "psM", "psA"))
        sem = lambda name: k.sem("s_" + name)
        consts, cleared, prefilled, sub_done, abs_done, w_mm, h_copied, hid_done, r_mm = (sem(n) for n in (
            "consts", "cleared", "prefilled", "sub_done", "abs_done", "w_mm", "h_copied", "hid_done", "r_mm"))
        rows_ready, turned, rot_ready, written, back, fwd_ready, m_mm, negmax, expd = (sem(n) for n in (
            "rows_ready", "turned", "rot_ready", "written", "back", "fwd_ready", "m_mm", "negmax", "expd"))
        recip, dg_ready, att_mm, att_ready, hg_ready, y_mm, y_ready, counted = (sem(n) for n in (
            "recip", "dg_ready", "att_mm", "att_ready", "hg_ready", "y_mm", "y_ready", "counted"))

        def graphs(eng, step):
            step(0, 0, True, False, False, False)
            step(1, 1, True, True, False, False)
            step(2, 0, True, True, True, False)
            with eng.Fori(0, (B - 4) // 2) as t:
                for u in (0, 1):
                    step(2 * t + (u + 3), 1 - u, True, True, True, True)
            step(B - 1, 1, True, True, True, True)
            step(B, 0, False, True, True, True)
            step(B + 1, 1, False, False, True, True)
            step(B + 2, 0, False, False, False, True)

        def behind(n, s, lag, zero, one):
            if s >= lag:
                return (n * SLABS + (s - lag), s - lag, n) if zero else None
            return (n * SLABS + (s - lag), s - lag + SLABS, n - 1) if one else None

        with nc.Block() as block:
            @block.sync
            def _(sp):
                sp.dma_start(dmask[:, :], k.a["c_dmask"]).then_inc(consts, 16)
                for p in (0, 1):
                    sp.dma_start(scratch[p].rearrange("(i j) -> i j", j=2 * N), diag0[:, :]).then_inc(prefilled, 16)
                sp.wait_ge(consts, 16)
                sp.wait_ge(prefilled, 32)

                def step(n, p, zero, one, two, three):
                    if not two:
                        return
                    m = n - 2
                    sp.wait_ge(rot_ready, done(m))
                    dst = scratch[p]
                    sp.dma_start(bass.AP(dst.tensor, dst.offset + 1, [[2 * N + 1, N], [1, HID]]), rot[:, p, :]).then_inc(written, 16)
                    sp.wait_ge(written, 16 * (n - 1))
                    sp.dma_start(wide[:, p, :], dst.rearrange("(i j) -> i j", j=2 * N)).then_inc(back, 16)
                graphs(sp, step)

            @block.gpsimd
            def _(pool):
                pool.sem_inc(hg_ready, BIAS)

                def step(n, p, zero, one, two, three):
                    if two:
                        m = n - 2
                        pool.wait_ge(y_mm, done(m - 2))
                        nc.gpsimd.tensor_copy(hg[:, p, :], hy[:, bass.ds(m * C, C)]).then_inc(hg_ready, 1)
                graphs(pool, step)

            @block.vector
            def _(dve):
                for s in (sub_done, hid_done, rot_ready, fwd_ready, negmax, recip, dg_ready, att_ready, counted):
                    dve.sem_inc(s, BIAS)
                nc.vector.memset(place[:].rearrange("r m c -> r (m c)"), 0.0).then_inc(cleared, 1)
                dve.wait_ge(cleared, 1)
                for m in (0, 1):
                    nc.vector.tensor_copy(place[0:HID, m, m:m + 1], k.pcol[0:HID, 3:4])
                    last = nc.vector.tensor_copy(place[HID:N, m, 2 + m:3 + m], k.pcol[HID:N, 3:4])
                last.then_inc(cleared, 1)
                dve.wait_ge(consts, 16)

                def subtract(n, s):
                    m = n * SLABS + s
                    dve.wait_ge(abs_done, done(m - 2))
                    one, far = windows(hd, n, s)
                    nc.vector.tensor_tensor(dif[:, s % 2, :].rearrange("c (h d i) -> c h d i", h=2, i=N), one, far,
                                            ALU.subtract).then_inc(sub_done, 1)

                def leaky(m, s):
                    dve.wait_ge(h_copied, done(m))
                    nc.vector.scalar_tensor_tensor(out=hid[:, s, :], in0=hid[:, s, :], scalar=0.01, in1=hid[:, s, :],
                                                   op0=ALU.mult, op1=ALU.max).then_inc(hid_done, 1)

                def step(n, p, zero, one, two, three):
                    q = 1 - p
                    for s in range(SLABS):
                        if zero:
                            subtract(n, s)
                        late = behind(n, s, 3, zero, one)
                        if late:
                            leaky(*late[0:2])
                        if s == 0 and two:
                            m = n - 2
                            dve.wait_ge(turned, done(m))
                            if three:
                                dve.wait_ge(written, 16 * (n - 3))
                            dve.wait_ge(fwd_ready, done(m - 2))
                            nc.vector.tensor_tensor(
                                rot[:, p, :].rearrange("i (s q d) -> i s q d", s=4, q=4),
                                psT[:, :].rearrange("i (d q s) -> i s q d", d=4, q=4)[:, 0:4],
                                dmask[:, :].rearrange("i (s q d) -> i s q d", s=4, q=4), ALU.mult).then_inc(rot_ready, 1)
                        if s == 2 and two:
                            m = n - 2
                            dve.wait_ge(back, 16 * (n - 1))
                            dve.wait_ge(m_mm, done(m - 2))
                            nc.vector.tensor_tensor(fwd[:, p, :], wide[:, p, 0:N], wide[:, p, N:2 * N], ALU.add).then_inc(fwd_ready, 1)
                        if s == 3 and two:
                            m = n - 2
                            dve.wait_ge(m_mm, done(m))
                            dve.wait_ge(expd, done(m - 2))
                            nc.vector.tensor_reduce(nmx[:, p:p + 1], psM[:, 0:N], AX.X, ALU.max, negate=True).then_inc(negmax, 1)
                        if s == 0 and three:
                            m = n - 3
                            dve.wait_ge(expd, done(m))
                            dve.wait_ge(dg_ready, done(m - 2))
                            nc.vector.reciprocal(rz[:, q:q + 1], zs[:, q:q + 1]).then_inc(recip, 1)
                            dve.wait_ge(recip, done(m))
                            dve.wait_ge(att_mm, done(m - 2))
                            nc.vector.tensor_scalar(dg[:, q, :], k.ident[:, :], rz[:, q:q + 1], None, ALU.mult).then_inc(dg_ready, 1)
                        if s == 1 and three:
                            m = n - 3
                            dve.wait_ge(att_mm, done(m))
                            dve.wait_ge(y_mm, done(m - 2))
                            nc.vector.tensor_copy(attT[:, q, :], psA[:, 0:N]).then_inc(att_ready, 1)
                        if s == 3 and three:
                            m = n - 3
                            dve.wait_ge(y_ready, done(m))
                            nc.vector.bn_stats(ystats[:, bass.ds(m, 1), :], hy[:, bass.ds(m * C, C)]).then_inc(counted, 1)
                graphs(dve, step)

            @block.scalar
            def _(act):
                for s in (abs_done, h_copied, rows_ready, expd, y_ready):
                    act.sem_inc(s, BIAS)

                def absolute(n, s):
                    m = n * SLABS + s
                    act.wait_ge(sub_done, done(m))
                    act.wait_ge(w_mm, done(m - 2))
                    nc.scalar.activation(D[:, s % 2, :], dif[:, s % 2, :], ACT.Abs).then_inc(abs_done, 1)

                def hidden(m, s):
                    act.wait_ge(w_mm, done(m))
                    act.wait_ge(r_mm, done(m - SLABS))
                    nc.scalar.activation(hid[:, s, :], psW[:, s % 2, :], ACT.Identity, bias=beta[:, 0:1],
                                         scale=alpha[:, 0:1]).then_inc(h_copied, 1)

                def step(n, p, zero, one, two, three):
                    q = 1 - p
                    for s in range(SLABS):
                        if s == 3 and one:
                            m = n - 1
                            act.wait_ge(r_mm, done(SLABS * n - 1))
                            act.wait_ge(turned, done(m - 1))
                            nc.scalar.activation(rows[:, :], psR[:, :], ACT.Identity, bias=k.pcol[:, 4:5]).then_inc(rows_ready, 1)
                        if zero:
                            absolute(n, s)
                        late = behind(n, s, 1, zero, one)
                        if late:
                            hidden(*late[0:2])
                        if s == 3 and two:
                            m = n - 2
                            act.wait_ge(negmax, done(m))
                            act.wait_ge(att_mm, done(m - 2))
                            act.wait_ge(recip, done(m - 2))
                            nc.scalar.activation(ex[:, p, :], psM[:, 0:N], ACT.Exp, bias=nmx[:, p:p + 1],
                                                 accum_out=zs[:, p:p + 1]).then_inc(expd, 1)
                        if s == 2 and three:
                            m = n - 3
                            act.wait_ge(y_mm, done(m))
                            act.wait_ge(hg_ready, done(m))
                            nc.scalar.activation(hy[:, bass.ds(m * C, C)], psA[:, 128:256], ACT.Identity,
                                                 bias=k.pcol[:, 5:6]).then_inc(y_ready, 1)
                graphs(act, step)

            @block.tensor
            def _(pe):
                for s in (w_mm, r_mm, turned, m_mm, att_mm, y_mm):
                    pe.sem_inc(s, BIAS)
                pe.wait_ge(cleared, 2)

                def product(n, s):
                    m = n * SLABS + s
                    pe.wait_ge(abs_done, done(m))
                    pe.wait_ge(h_copied, done(m - 2))
                    pair_product(nc, k, psW[:, s % 2, :], D[:, s % 2, :]).then_inc(w_mm, 1)

                def second(m, s, n):
                    pe.wait_ge(hid_done, done(m))
                    if s == 0:
                        pe.wait_ge(rows_ready, done(n - 1))
                    for c in (0, 1):
                        at, q = divmod(2 * s + c, 4)
                        last = nc.tensor.matmul(psR[32 * q:32 * q + 32, :], place[:, at, :], hid[:, s, c * 512:(c + 1) * 512],
                                                start=at == 0, stop=at == 1)
                    last.then_inc(r_mm, 1)

                def step(n, p, zero, one, two, three):
                    q = 1 - p
                    for s in range(SLABS):
                        if zero:
                            product(n, s)
                        late = behind(n, s, 3, zero, one)
                        if late:
                            second(*late)
                        if s == 3 and one:
                            m = n - 1
                            pe.wait_ge(rows_ready, done(m))
                            pe.wait_ge(rot_ready, done(m - 1))
                            for d in range(4):
                                last = nc.tensor.transpose(psT[:, d * N:(d + 1) * N], rows[:, d * N:(d + 1) * N], k.ident[:, :])
                            last.then_inc(turned, 1)
                        if s == 2 and two:
                            m = n - 2
                            pe.wait_ge(fwd_ready, done(m))
                            pe.wait_ge(expd, done(m - 1))
                            nc.tensor.matmul(psM[:, 0:N], k.ident[:, :], fwd[:, p, :], start=True, stop=False)
                            nc.tensor.matmul(psM[:, 0:N], fwd[:, p, :], k.ident[:, :], start=False, stop=False)
                            nc.tensor.matmul(psM[:, 0:N], k.identb[:, :], k.negm[:, bass.ds(m * N, N)], start=False,
                                             stop=True).then_inc(m_mm, 1)
                        if s == 0 and three:
                            m = n - 3
                            pe.wait_ge(dg_ready, done(m))
                            pe.wait_ge(expd, done(m))
                            pe.wait_ge(y_ready, done(m - 1))
                            nc.tensor.matmul(psA[:, 0:N], ex[:, q, :], dg[:, q, :], start=True, stop=True).then_inc(att_mm, 1)
                        if s == 1 and three:
                            m = n - 3
                            pe.wait_ge(att_ready, done(m))
                            pe.wait_ge(hg_ready, done(m))
                            nc.tensor.matmul(psA[:, 128:256], hg[:, q, :], attT[:, q, :], start=True, stop=True).then_inc(y_mm, 1)
                graphs(pe, step)


def phase_output(nc, k, hd, hy, ystats, out):
    with ExitStack() as ctx:
        sb = lambda name, shape, dt=F32: k.sb(ctx, "o_" + name, shape, dt)
        mv = sb("mv", [C, 2])
        v = sb("v", [C, 6])
        hq = sb("hq", [C, 2, QC])
        yn = sb("yn", [C, 2, QC])
        t1 = sb("t1", [N, 2, QC])
        res = sb("res", [N, 2, QC])
        psU = k.ps(ctx, "o_psU", [N, 2, 512])
        sem = lambda name: k.sem("o_" + name)
        algebra, rooted, scaled, leaky, h_copied, u_mm, biased, res_ready = (sem(n) for n in (
            "algebra", "rooted", "scaled", "leaky", "h_copied", "u_mm", "biased", "res_ready"))
        stored = [sem("stored0"), sem("stored1")]
        b = lambda i: slice(i * N, (i + 1) * N)

        def quads(eng, step):
            with eng.Fori(0, QUADS // 2) as t:
                for u in (0, 1):
                    step(2 * t + u, u, t)

        with nc.Block() as block:
            @block.vector
            def _(dve):
                for s in (leaky, biased, res_ready):
                    dve.sem_inc(s, BIAS)
                at = [0]

                def link(ins):
                    at[0] += 1
                    ins.then_inc(algebra, 1)
                    dve.wait_ge(algebra, at[0])
                c = lambda i: v[:, i:i + 1]
                gg, beg = k.pcol[:, 6:7], k.pcol[:, 7:8]
                link(nc.vector.bn_aggr(mv[:, :], ystats[:].rearrange("c b s -> c (b s)")))
                link(nc.vector.tensor_scalar(c(0), mv[:, 1:2], EPS, None, ALU.add))
                dve.wait_ge(rooted, 1)
                link(nc.vector.reciprocal(c(2), c(1)))
                link(nc.vector.tensor_tensor(c(3), c(2), gg, ALU.mult))
                link(nc.vector.tensor_tensor(c(4), mv[:, 0:1], c(3), ALU.mult))
                link(nc.vector.tensor_tensor(c(5), beg, c(4), ALU.subtract))

                def step(g, p, t):
                    dve.wait_ge(scaled, done(g))
                    nc.vector.scalar_tensor_tensor(out=yn[:, p, :], in0=yn[:, p, :], scalar=0.01, in1=yn[:, p, :],
                                                   op0=ALU.mult, op1=ALU.max).then_inc(leaky, 1)
                    dve.wait_ge(u_mm, done(g))
                    dve.wait_ge(res_ready, done(g - 2))
                    nc.vector.tensor_tensor(
                        t1[:, p, :].rearrange("n (b c) -> n b c", c=C), psU[:, p, :].rearrange("n (b c) -> n b c", c=C),
                        k.bt[:, :].unsqueeze(1).broadcast_to([N, G, C]), ALU.add).then_inc(biased, 1)
                    dve.wait_ge(biased, done(g))
                    dve.wait_ge(stored[p], 16 * t + 16)
                    nc.vector.tensor_tensor(res[:, p, :], t1[:, p, :], k.x[:, bass.ds(g * QC, QC)], ALU.add).then_inc(res_ready, 1)
                quads(dve, step)

            @block.gpsimd
            def _(pool):
                pool.sem_inc(h_copied, BIAS)

                def step(g, p, t):
                    pool.wait_ge(u_mm, done(g - 2))
                    nc.gpsimd.tensor_copy(
                        hq[:, p, :].rearrange("c (b n) -> c b n", n=N),
                        hd[:, bass.ds(g * (G * DUP), G * DUP)].rearrange("c (b n) -> c b n", n=DUP)[:, :, 0:N]).then_inc(h_copied, 1)
                quads(pool, step)

            @block.scalar
            def _(act):
                act.sem_inc(scaled, BIAS)
                act.wait_ge(algebra, 2)
                nc.scalar.activation(v[:, 1:2], v[:, 0:1], ACT.Sqrt).then_inc(rooted, 1)
                act.wait_ge(algebra, 6)

                def step(g, p, t):
                    act.wait_ge(u_mm, done(g - 2))
                    nc.scalar.activation(yn[:, p, :], hy[:, bass.ds(g * QC, QC)], ACT.Identity, bias=v[:, 5:6],
                                         scale=v[:, 3:4]).then_inc(scaled, 1)
                quads(act, step)

            @block.tensor
            def _(pe):
                pe.sem_inc(u_mm, BIAS)

                def step(g, p, t):
                    pe.wait_ge(h_copied, done(g))
                    pe.wait_ge(leaky, done(g))
                    pe.wait_ge(biased, done(g - 2))
                    for i in range(G):
                        nc.tensor.matmul(psU[:, p, b(i)], hq[:, p, b(i)], k.wtT[:, 0, :], start=True, stop=False)
                        last = nc.tensor.matmul(psU[:, p, b(i)], yn[:, p, b(i)], k.wtT[:, 1, :], start=False, stop=True)
                    last.then_inc(u_mm, 1)
                quads(pe, step)

            @block.sync
            def _(sp):
                for p in (0, 1):
                    sp.sem_inc(stored[p], 16)

                for g in range(QUADS):
                    sp.wait_ge(res_ready, done(g))
                    sp.dma_start(out[g * G:(g + 1) * G].rearrange("b n c -> n b c"),
                                 res[:, g % 2, :].rearrange("n (b c) -> n b c", c=C)).then_inc(stored[g % 2], 16)
                for p in (0, 1):
                    sp.wait_ge(stored[p], 16 * (QUADS // 2) + 16)


_INS = ['x', 'adj', 'nodemask', 'L0_gnn_W', 'L0_gnn_b', 'L0_gnn_a', 'L1_gnn_W1', 'L1_gnn_b1', 'L1_gnn_W2', 'L1_gnn_b2',
        'L1_gnn_Wu', 'L1_gnn_bu', 'L2_gnn_W', 'L2_gnn_a_w', 'L2_gnn_a_b', 'L3_gnn_W1', 'L3_gnn_b1', 'L3_gnn_g1',
        'L3_gnn_be1', 'L3_gnn_W2', 'L3_gnn_b2', 'L3_gnn_Wg', 'L3_gnn_bg', 'L3_gnn_gg', 'L3_gnn_beg', 'L3_gnn_Wt',
        'L3_gnn_bt']


def kernel(**inputs):
    import numpy as _np
    import concourse.bacc as _bacc
    from concourse import mybir as _mybir
    from concourse.bass_utils import run_bass_kernel_spmd as _run

    nc = _bacc.Bacc("TRN2", target_bir_lowering=False, num_devices=1)
    arrays, args = {}, {}
    given = {name: _np.ascontiguousarray(inputs[name]) for name in _INS}
    for name, v in {**given, **constants()}.items():
        arrays[f"in_{name}_dram"] = v
        args[name] = nc.dram_tensor(f"in_{name}_dram", v.shape, _mybir.dt.from_np(v.dtype), kind="ExternalInput").ap()
    out = nc.dram_tensor("out_0_dram", (B, N, C), _mybir.dt.float32, kind="ExternalOutput").ap()
    build(nc, args, out)
    r = _run(nc, [arrays], core_ids=[0])
    return r.results[0]["out_0_dram"]
```

```python
from contextlib import ExitStack

import numpy as np
import concourse.bass as bass
from concourse import mybir

ALU = mybir.AluOpType
ACT = mybir.ActivationFunctionType
F32 = mybir.dt.float32
BF16 = mybir.dt.bfloat16
I32 = mybir.dt.int32
AX = mybir.AxisListType

B, N, C = 64, 128, 128
G = 4
QUADS = B // G
QC = G * N
EPS = 1e-5
BIG = float(2.0 ** 60)
LOWEST = -3.0e38
HEADS = 8
BLK = 6
NBLK = (N + BLK - 1) // BLK
SUB = 2 ** BLK
NCH = NBLK // 2
NG = (NCH + 3) // 4
HID = C // 2
BIAS = 12


def done(n):
    return n + 1 + BIAS


def constants():
    bf = mybir.dt.np(BF16)
    subset = np.arange(SUB)
    sel = np.zeros((N, NBLK * SUB), np.float32)
    for j in range(N):
        blk, t = divmod(j, BLK)
        sel[j, blk * SUB:(blk + 1) * SUB] = 2.0 * ((subset >> t) & 1) - 1.0
    nhot = 1.0 - sum((subset >> t) & 1 for t in range(BLK))
    blockind = np.zeros((HEADS, HEADS * N), np.float32)
    for h in range(HEADS):
        blockind[h, h * N:(h + 1) * N] = 1.0
    dmask = np.ones((N, HID), np.float32)
    dmask[N // 2:, HID - 1] = 0.0
    linrows = np.isin(np.arange(N) % 32, (1, 3)).astype(np.float32).reshape(N, 1)
    return {
        "c_linrows": linrows,
        "c_ident": np.eye(N, dtype=np.float32),
        "c_identb": np.eye(N, dtype=np.float32).astype(bf),
        "c_sel": sel.astype(bf),
        "c_blockind": blockind,
        "c_nhot": np.tile(nhot, 2).astype(np.float32).reshape(N, 1),
        "c_dmask": dmask,
        "c_fold": np.tile(np.eye(HID, dtype=np.float32), (2, 2)),
    }


class Parts:
    pass


def build(nc, a, out):
    with ExitStack() as ctx:
        k = Parts()
        k.a = a
        k.sb = lambda c, name, shape, dt: c.enter_context(nc.sbuf_tensor(name, shape, dt))
        k.ps = lambda c, name, shape, dt=F32: c.enter_context(nc.psum_tensor(name, shape, dt))
        k.sem = lambda name: ctx.enter_context(nc.semaphore(name))
        sb = lambda name, shape, dt=F32: k.sb(ctx, name, shape, dt)
        k.x = sb("x_all", [N, B * C])
        k.negm = sb("negm", [N, B * N], BF16)
        k.ident = sb("ident", [N, N])
        k.identb = sb("identb", [N, N], BF16)
        k.stats = sb("ln_stats", [N, B, 6])
        k.nmean = sb("ln_negmean", [N, B])
        k.rstd = sb("ln_rstd", [N, B])
        k.nmT = sb("nodemask_cols", [N, B])
        k.w0 = sb("w0", [C, C])
        k.wsrc = sb("wa_src_bc", [C, N])
        k.wdst = sb("wa_dst_bc", [C, N])
        k.b0 = sb("b0_bc", [N, C])
        k.c0 = sb("b0_dot_a", [N, 1])
        k.w1T = sb("l1_w1T", [C, C])
        k.w2T = sb("l1_w2T", [C, C])
        k.b1 = sb("l1_b1", [C, 1])
        k.b2 = sb("l1_b2", [C, 1])
        k.wuT = sb("l1_wuT", [C, 2, C])
        k.bu = sb("l1_bu_bc", [N, C])
        k.wl2 = sb("l2_w", [C, C])
        k.wa = sb("l2_wa", [C, 2, HEADS])
        k.ab = sb("l2_ab", [HEADS, 1])
        k.p1T = sb("l3_w1T", [C, HID])
        k.pcol = sb("l3_cols", [N, 8])
        k.wgT = sb("l3_wgT", [C, C])
        k.wtT = sb("l3_wtT", [C, 2, C])
        k.bt = sb("l3_bt_bc", [N, C])
        with ExitStack() as mask_ctx:
            k.mask1 = k.sb(mask_ctx, "mask1", [N, B * N], BF16)
            phase_load(nc, k, a)
            phase_gat(nc, k)
            phase_maxpass(nc, k)
        phase_heads(nc, k)
        phase_pairs(nc, k, a, out)


def phase_load(nc, k, a):
    with ExitStack() as ctx:
        raw = k.sb(ctx, "w_raw", [N, 10, N], F32)
        acol = k.sb(ctx, "a_cols", [C, 2], F32)
        b0col = k.sb(ctx, "b0_col", [C, 1], F32)
        b0mat = k.sb(ctx, "b0_mat", [C, N], F32)
        ones = k.sb(ctx, "w_ones", [N, N], F32)
        w0T = k.sb(ctx, "w0T", [C, C], F32)
        l2wT = k.sb(ctx, "l2_wT", [C, C], F32)
        aT = k.sb(ctx, "l2_aT", [C, 2, HEADS], F32)
        wacol = k.sb(ctx, "wa_cols", [C, 2], F32)
        ps = k.ps(ctx, "w_ps", [N, 8, 512])
        loaded, turned, copied, folded, spread = (k.sem(n) for n in (
            "w_loaded", "w_turned", "w_copied", "w_folded", "w_spread"))
        n_load = [0]
        DEPTH = 4
        ring = k.sb(ctx, "adj_ring", [N, DEPTH, QC], I32)
        masked = k.sem("masked")
        x_in = [k.sem(f"x_in{i}") for i in range(DEPTH)]
        adj_in = [k.sem(f"adj_in{i}") for i in range(DEPTH)]
        turns = [
            (a["L0_gnn_W"], N, w0T[:, :]), (a["L1_gnn_W1"], N, k.w1T[:, :]), (a["L1_gnn_W2"], N, k.w2T[:, :]),
            (a["L1_gnn_Wu"][:, 0:C], N, k.wuT[:, 0, :]), (a["L1_gnn_Wu"][:, C:2 * C], N, k.wuT[:, 1, :]),
            (a["L2_gnn_W"], N, l2wT[:, :]), (a["L3_gnn_W1"], HID, k.p1T[:, :]), (a["L3_gnn_Wg"], N, k.wgT[:, :]),
            (a["L3_gnn_Wt"][:, 0:C], N, k.wtT[:, 0, :]), (a["L3_gnn_Wt"][:, C:2 * C], N, k.wtT[:, 1, :]),
        ]
        a2raw = k.sb(ctx, "l2_a_raw", [HEADS, 2 * C], F32)
        nmraw = k.sb(ctx, "nodemask_raw", [B, N], F32)
        col = lambda v, n: v.rearrange("(p o) -> p o", o=1)[0:n]
        row = lambda v, n: v.rearrange("(o c) -> o c", o=1).broadcast_to([n, v.shape[0]])
        with nc.Block() as block:
            @block.sync
            def _(sp):
                def load(dst, src):
                    sp.dma_start(dst, src).then_inc(loaded, 16)
                    n_load[0] += 1
                load(k.ident[:, :], a["c_ident"])
                load(k.identb[:, :], a["c_identb"])
                for i, (src, rows, _) in enumerate(turns):
                    load(raw[0:rows, i, :], src)
                load(a2raw[:, :], a["L2_gnn_a_w"])
                load(nmraw[:, :], a["nodemask"])
                load(k.w0[:, :], a["L0_gnn_W"])
                load(k.wl2[:, :], a["L2_gnn_W"])
                load(acol[:, 0:1], col(a["L0_gnn_a"][0:C], C))
                load(acol[:, 1:2], col(a["L0_gnn_a"][C:2 * C], C))
                load(b0col[:, :], col(a["L0_gnn_b"], C))
                load(k.b1[:, :], col(a["L1_gnn_b1"], C))
                load(k.b2[:, :], col(a["L1_gnn_b2"], C))
                load(k.ab[:, :], col(a["L2_gnn_a_b"], HEADS))
                load(k.b0[:, :], row(a["L0_gnn_b"], N))
                load(k.bu[:, :], row(a["L1_gnn_bu"], N))
                load(k.bt[:, :], row(a["L3_gnn_bt"], N))
                for half in (0, HID):
                    rows = slice(half, half + HID)
                    load(k.pcol[rows, 0:1], col(a["L3_gnn_b1"], HID))
                    load(k.pcol[rows, 1:2], col(a["L3_gnn_g1"], HID))
                    load(k.pcol[rows, 2:3], col(a["L3_gnn_be1"], HID))
                    load(k.pcol[rows, 3:4], a["L3_gnn_W2"].rearrange("o c -> c o"))
                load(k.pcol[:, 4:5], a["L3_gnn_b2"].rearrange("(o c) -> o c", o=1).broadcast_to([N, 1]))
                load(k.pcol[:, 5:6], col(a["L3_gnn_bg"], C))
                load(k.pcol[:, 6:7], col(a["L3_gnn_gg"], C))
                load(k.pcol[:, 7:8], col(a["L3_gnn_beg"], C))
                sp.wait_ge(loaded, 16 * n_load[0])

            @block.scalar
            def _(act):
                for g in range(QUADS):
                    if g >= DEPTH:
                        act.wait_ge(masked, g - DEPTH + 1)
                        act.wait_ge(x_in[g % DEPTH], 16 * (g // DEPTH))
                    act.dma_start(ring[:, g % DEPTH, :].rearrange("n (b c) -> n b c", c=N),
                                  a["adj"][g * G:(g + 1) * G].rearrange("b n m -> n b m")).then_inc(adj_in[g % DEPTH], 16)
                    act.dma_start(k.x[:, g * QC:(g + 1) * QC].rearrange("n (b c) -> n b c", c=C),
                                  a["x"][g * G:(g + 1) * G].rearrange("b n c -> n b c")).then_inc(x_in[g % DEPTH], 16)

            @block.tensor
            def _(pe):
                pe.wait_ge(loaded, 16 * n_load[0])
                for i, (_, rows, _) in enumerate(turns):
                    last = nc.tensor.transpose(ps[:, i // 4, (i % 4) * N:(i % 4) * N + rows], raw[0:rows, i, :],
                                               k.ident[0:rows, 0:rows])
                for s in (0, 1):
                    nc.tensor.transpose(ps[:, 3, s * HEADS:(s + 1) * HEADS], a2raw[:, s * C:(s + 1) * C],
                                        k.ident[0:HEADS, 0:HEADS])
                nc.tensor.transpose(ps[:, 3, N:N + B], nmraw[:, :], k.ident[0:B, 0:B]).then_inc(turned, 1)
                pe.wait_ge(copied, 1)
                nc.tensor.matmul(ps[:, 4, 0:2], w0T[:, :], acol[:, :], start=True, stop=True)
                nc.tensor.matmul(ps[:, 5, 0:2 * HEADS], l2wT[:, :], aT[:].rearrange("c s h -> c (s h)"), start=True, stop=True)
                nc.tensor.matmul(ps[:, 6, 0:2], b0mat[:, :], acol[:, :], start=True, stop=True).then_inc(folded, 1)

            @block.vector
            def _(dve):
                def take(g):
                    cols = slice(g * QC, (g + 1) * QC)
                    dve.wait_ge(adj_in[g % DEPTH], 16 * (g // DEPTH + 1))
                    nc.vector.tensor_scalar(k.negm[:, cols], ring[:, g % DEPTH, :], 0, -BIG, ALU.is_le, ALU.mult)
                    nc.vector.tensor_scalar(k.mask1[:, cols], ring[:, g % DEPTH, :], 0, None, ALU.not_equal).then_inc(masked, 1)
                    dve.wait_ge(x_in[g % DEPTH], 16 * (g // DEPTH + 1))
                    ln_stats(nc, k, g)

                EARLY = QUADS - 4
                for g in range(EARLY):
                    take(g)
                dve.wait_ge(loaded, 16 * n_load[0])
                nc.vector.memset(ones[:, :], 1.0).then_inc(spread, 1)
                dve.wait_ge(spread, 1)
                nc.vector.tensor_scalar(b0mat[:, :], ones[:, :], b0col[:, 0:1], None, ALU.mult)
                take(EARLY)
                dve.wait_ge(turned, 1)
                for i, (_, rows, dst) in enumerate(turns):
                    nc.vector.tensor_copy(dst, ps[:, i // 4, (i % 4) * N:(i % 4) * N + rows])
                nc.vector.tensor_copy(aT[:].rearrange("c s h -> c (s h)"), ps[:, 3, 0:2 * HEADS])
                nc.vector.tensor_copy(k.nmT[:, :], ps[:, 3, N:N + B]).then_inc(copied, 1)
                take(EARLY + 1)
                dve.wait_ge(folded, 1)
                nc.vector.tensor_copy(wacol[:, :], ps[:, 4, 0:2])
                nc.vector.tensor_copy(k.wa[:].rearrange("c s h -> c (s h)"), ps[:, 5, 0:2 * HEADS])
                nc.vector.tensor_reduce(k.c0[:, :], ps[:, 6, 0:2], AX.X, ALU.add).then_inc(spread, 1)
                dve.wait_ge(spread, 2)
                nc.vector.tensor_scalar(k.wsrc[:, :], ones[:, :], wacol[:, 0:1], None, ALU.mult)
                nc.vector.tensor_scalar(k.wdst[:, :], ones[:, :], wacol[:, 1:2], None, ALU.mult)
                for g in range(EARLY + 2, QUADS):
                    take(g)


def ln_stats(nc, k, g):
    for i in range(G):
        nc.vector.bn_stats(k.stats[:, bass.ds(g * G + i, 1), :], k.x[:, bass.ds((g * G + i) * C, C)])


def phase_norm(nc, k, tag):
    with ExitStack() as ctx:
        sb = lambda name: k.sb(ctx, f"{tag}_{name}", [N, B], F32)
        msum, mdif, squares, within, apart, ve, sd = (sb(n) for n in (
            "mean_sum", "mean_dif", "squares", "within", "apart", "var_eps", "std"))
        halves, parts, eps_added, rooted = (k.sem(f"{tag}_{n}") for n in ("halves", "parts", "eps_added", "rooted"))
        with nc.Block() as block:
            @block.vector
            def _(dve):
                mean = (k.stats[:, :, 1], k.stats[:, :, 4])
                summed = (k.stats[:, :, 2], k.stats[:, :, 5])
                nc.vector.tensor_tensor(msum[:, :], mean[0], mean[1], ALU.add)
                nc.vector.tensor_tensor(mdif[:, :], mean[0], mean[1], ALU.subtract)
                nc.vector.tensor_tensor(squares[:, :], summed[0], summed[1], ALU.add).then_inc(halves, 1)
                dve.wait_ge(halves, 1)
                nc.vector.tensor_scalar(k.nmean[:, :], msum[:, :], -0.5, None, ALU.mult)
                nc.vector.tensor_scalar(within[:, :], squares[:, :], 1.0 / C, EPS, ALU.mult, ALU.add)
                nc.vector.tensor_tensor(apart[:, :], mdif[:, :], mdif[:, :], ALU.mult).then_inc(parts, 1)
                dve.wait_ge(parts, 1)
                nc.vector.scalar_tensor_tensor(out=ve[:, :], in0=apart[:, :], scalar=0.25, in1=within[:, :],
                                               op0=ALU.mult, op1=ALU.add).then_inc(eps_added, 1)
                dve.wait_ge(rooted, 1)
                nc.vector.reciprocal(k.rstd[:, :], sd[:, :])

            @block.scalar
            def _(act):
                act.wait_ge(eps_added, 1)
                nc.scalar.activation(sd[:, :], ve[:, :], ACT.Sqrt).then_inc(rooted, 1)


def quad_rows(v):
    return v.rearrange("n (b c) -> n b c", c=C)


def per_row(v, g):
    return v[:, bass.ds(g * G, G)].unsqueeze(2).broadcast_to([N, G, C])


def normalize_center(nc, k, xn, g, centered):
    nc.gpsimd.tensor_tensor(quad_rows(xn), quad_rows(k.x[:, bass.ds(g * QC, QC)]), per_row(k.nmean, g),
                            ALU.add).then_inc(centered, 1)


def normalize_scale(nc, k, xn, g, normed):
    nc.gpsimd.tensor_tensor(quad_rows(xn), quad_rows(xn), per_row(k.rstd, g), ALU.mult).then_inc(normed, 1)


def normalize(nc, k, pool, xn, g, centered, normed):
    normalize_center(nc, k, xn, g, centered)
    pool.wait_ge(centered, done(g))
    normalize_scale(nc, k, xn, g, normed)


def phase_gat(nc, k):
    phase_norm(nc, k, "n0")
    with ExitStack() as ctx:
        sb = lambda name, shape, dt=F32: k.sb(ctx, "g_" + name, shape, dt)
        xn = sb("xn", [N, 2, QC])
        hT = sb("hT", [C, 2, QC])
        hs = sb("h", [N, B * C])
        el = sb("el", [N, 2, QC])
        ex = sb("ex", [N, 2, QC])
        exT = sb("exT", [N, 2, QC])
        nmx = sb("nmx", [N, 2, G])
        zs = sb("zs", [N, 2, G])
        rz = sb("rz", [N, 2, G])
        rzm = sb("rz_masked", [N, 2, G])
        psT, psH, psE, psD, psO = (k.ps(ctx, "g_" + n, [N, QC]) for n in ("psT", "psH", "psE", "psD", "psO"))
        sem = lambda name: k.sem("g_" + name)
        centered, normed, transposed, relued, h_mm, h_ready, e_mm, e_copied, leaky, negmax, expd = (sem(n) for n in (
            "centered", "normed", "transposed", "relued", "h_mm", "h_ready", "e_mm", "e_copied", "leaky", "negmax", "expd"))
        ex_turned, exT_ready, recip, scaled, out_mm, added = (sem(n) for n in (
            "ex_turned", "exT_ready", "recip", "scaled", "out_mm", "added"))
        b = lambda i: slice(i * N, (i + 1) * N)

        def slots(eng, slot):
            def peeled(g):
                slot(g, g % 2, lambda lag: 0 <= g - lag < QUADS)
            for g in range(4):
                peeled(g)
            with eng.Fori(0, (QUADS - 6) // 2) as t:
                for u in (0, 1):
                    slot(2 * t + (u + 4), u, lambda lag: True)
            for g in range(QUADS - 2, QUADS + 4):
                peeled(g)

        with nc.Block() as block:
            @block.gpsimd
            def _(pool):
                for s in (centered, normed):
                    pool.sem_inc(s, BIAS)

                def step(g, p):
                    pool.wait_ge(transposed, done(g - 2))
                    normalize(nc, k, pool, xn[:, p, :], g, centered, normed)
                with pool.Fori(0, QUADS // 2) as t:
                    for u in (0, 1):
                        step(2 * t + u, u)

            @block.tensor
            def _(pe):
                for s in (transposed, h_mm, e_mm, ex_turned, out_mm):
                    pe.sem_inc(s, BIAS)

                def turn(g, p):
                    pe.wait_ge(normed, done(g))
                    pe.wait_ge(relued, done(g - 1))
                    for i in range(G):
                        last = nc.tensor.transpose(psT[:, b(i)], xn[:, p, b(i)], k.ident[:, :])
                    last.then_inc(transposed, 1)

                def slot(g, p, exists):
                    q = 1 - p
                    if exists(4):
                        m = g - 4
                        pe.wait_ge(exT_ready, done(m))
                        pe.wait_ge(h_ready, done(m))
                        pe.wait_ge(added, done(m - 1))
                        for i in range(G):
                            last = nc.tensor.matmul(psO[:, b(i)], exT[:, p, b(i)], hs[:, bass.ds((m * G + i) * C, C)],
                                                    start=True, stop=True)
                        last.then_inc(out_mm, 1)
                    if exists(3):
                        m = g - 3
                        pe.wait_ge(expd, done(m))
                        pe.wait_ge(exT_ready, done(m - 1))
                        for i in range(G):
                            last = nc.tensor.transpose(psD[:, b(i)], ex[:, q, b(i)], k.ident[:, :])
                        last.then_inc(ex_turned, 1)
                    if exists(0):
                        pe.wait_ge(relued, done(g))
                        pe.wait_ge(h_ready, done(g - 1))
                        for i in range(G):
                            last = nc.tensor.matmul(psH[:, b(i)], hT[:, p, b(i)], k.w0[:, :], start=True, stop=True)
                        last.then_inc(h_mm, 1)
                        pe.wait_ge(e_copied, done(g - 1))
                        nc.tensor.matmul(psE[:, :], k.wdst[:, :], hT[:, p, :], start=True, stop=False)
                        nc.tensor.matmul(psE[:, :], k.identb[:, :], k.negm[:, bass.ds(g * QC, QC)], start=False, stop=False)
                        for i in range(G):
                            last = nc.tensor.matmul(psE[:, b(i)], hT[:, p, b(i)], k.wsrc[:, :], start=False, stop=i == G - 1)
                        last.then_inc(e_mm, 1)
                    if exists(-1):
                        turn(g + 1, q)
                turn(0, 0)
                slots(pe, slot)

            @block.scalar
            def _(act):
                for s in (relued, e_copied, expd):
                    act.sem_inc(s, BIAS)

                def relu(g, p):
                    act.wait_ge(transposed, done(g))
                    act.wait_ge(e_mm, done(g - 2))
                    nc.scalar.activation(hT[:, p, :], psT[:, :], ACT.Relu).then_inc(relued, 1)

                def slot(g, p, exists):
                    if exists(2):
                        m = g - 2
                        act.wait_ge(negmax, done(m))
                        act.wait_ge(ex_turned, done(m - 2))
                        act.wait_ge(recip, done(m - 2))
                        for i in range(G):
                            last = nc.scalar.activation(ex[:, p, b(i)], el[:, p, b(i)], ACT.Exp, bias=nmx[:, p, i:i + 1],
                                                        accum_out=zs[:, p, i:i + 1])
                        last.then_inc(expd, 1)
                    if exists(0):
                        act.wait_ge(e_mm, done(g))
                        act.wait_ge(expd, done(g - 2))
                        nc.scalar.activation(el[:, p, :], psE[:, :], ACT.Identity, bias=k.c0[:, 0:1]).then_inc(e_copied, 1)
                    if exists(-1):
                        relu(g + 1, 1 - p)
                relu(0, 0)
                slots(act, slot)

            @block.vector
            def _(dve):
                for s in (h_ready, leaky, negmax, exT_ready, recip, scaled, added):
                    dve.sem_inc(s, BIAS)

                def slot(g, p, exists):
                    q = 1 - p
                    if exists(3):
                        m = g - 3
                        dve.wait_ge(expd, done(m))
                        dve.wait_ge(scaled, done(m - 2))
                        nc.vector.reciprocal(rz[:, q, :], zs[:, q, :]).then_inc(recip, 1)
                        dve.wait_ge(recip, done(m))
                        dve.wait_ge(added, done(m - 2))
                        nc.vector.tensor_tensor(rzm[:, q, :], rz[:, q, :], k.nmT[:, bass.ds(m * G, G)], ALU.mult).then_inc(scaled, 1)
                    if exists(1):
                        m = g - 1
                        dve.wait_ge(e_copied, done(m))
                        nc.vector.scalar_tensor_tensor(out=el[:, q, :], in0=el[:, q, :], scalar=0.01, in1=el[:, q, :],
                                                       op0=ALU.mult, op1=ALU.max).then_inc(leaky, 1)
                        dve.wait_ge(leaky, done(m))
                        dve.wait_ge(expd, done(m - 2))
                        nc.vector.tensor_reduce(nmx[:, q, :], el[:, q, :].rearrange("n (b c) -> n b c", c=N), AX.X, ALU.max,
                                                negate=True).then_inc(negmax, 1)
                    if exists(4):
                        m = g - 4
                        dve.wait_ge(scaled, done(m))
                        dve.wait_ge(out_mm, done(m))
                        for i in range(G):
                            xs = k.x[:, bass.ds((m * G + i) * C, C)]
                            last = nc.vector.scalar_tensor_tensor(out=xs, in0=psO[:, b(i)], scalar=rzm[:, p, i:i + 1], in1=xs,
                                                                  op0=ALU.mult, op1=ALU.add)
                        last.then_inc(added, 1)
                    if exists(3):
                        m = g - 3
                        dve.wait_ge(ex_turned, done(m))
                        dve.wait_ge(out_mm, done(m - 2))
                        nc.vector.tensor_copy(exT[:, q, :], psD[:, :]).then_inc(exT_ready, 1)
                    if exists(4):
                        m = g - 4
                        dve.wait_ge(added, done(m))
                        ln_stats(nc, k, m)
                    if exists(0):
                        dve.wait_ge(h_mm, done(g))
                        nc.vector.tensor_tensor(
                            hs[:, bass.ds(g * QC, QC)].rearrange("n (b c) -> n b c", c=C),
                            psH[:, :].rearrange("n (b c) -> n b c", c=C),
                            k.b0[:, :].unsqueeze(1).broadcast_to([N, G, C]), ALU.add).then_inc(h_ready, 1)
                slots(dve, slot)


def phase_maxpass(nc, k):
    phase_norm(nc, k, "n1")
    with ExitStack() as ctx:
        sb = lambda name, shape, dt=F32: k.sb(ctx, "m_" + name, shape, dt)
        PADN = NBLK * BLK
        xn = sb("xn", [N, 2, QC])
        hT = sb("hT", [C, 2, QC])
        m1 = sb("m1", [C, 2, QC])
        m2 = sb("m2", [C, 2, G, PADN])
        table = sb("table", [C, G, NBLK, SUB])
        tableT = sb("tableT", [N, 2, 4, C])
        onehot = sb("onehot", [N, 2, 4, N])
        part = sb("part", [C, G, NG, N])
        mx = sb("mx", [C, QC])
        mT = sb("mT", [C, 2, QC])
        upd = sb("upd", [N, QC])
        sel = sb("sel", [N, NCH * 128], BF16)
        nhot = sb("nhot", [N, 1])
        psF, psTT, psC, psU = (k.ps(ctx, "m_" + n, [N, QC]) for n in ("psF", "psTT", "psC", "psU"))
        psS = k.ps(ctx, "m_psS", [N, 4, 512])
        sem = lambda name: k.sem("m_" + name)
        consts, padded, centered, normed, transposed, relued, m2_mm, m2_copied, m1_mm, m1_copied = (sem(n) for n in (
            "consts", "padded", "centered", "normed", "transposed", "relued", "m2_mm", "m2_copied", "m1_mm", "m1_copied"))
        grown, tabled, t_turned, tT_ready, match_mm, onehot_ready = (sem(n) for n in (
            "grown", "tabled", "t_turned", "tT_ready", "match_mm", "onehot_ready"))
        selected, reduced, merged, summed, mT_ready, u_mm, biased, added = (sem(n) for n in (
            "selected", "reduced", "merged", "summed", "mT_ready", "u_mm", "biased", "added"))
        b = lambda i: slice(i * N, (i + 1) * N)
        ITEMS = G * NG

        def quads(eng, quad):
            quad(0, 0, False, True)
            with eng.Fori(0, QUADS // 2 - 1) as t:
                for u in (0, 1):
                    quad(2 * t + (u + 1), 1 - u, True, True)
            quad(QUADS - 1, 1, True, False)

        with nc.Block() as block:
            @block.sync
            def _(sp):
                sp.dma_start(sel[:, :], k.a["c_sel"]).then_inc(consts, 16)
                sp.dma_start(nhot[:, :], k.a["c_nhot"]).then_inc(consts, 16)
                sp.wait_ge(consts, 32)

            @block.gpsimd
            def _(pool):
                for s in (centered, normed):
                    pool.sem_inc(s, BIAS)

                def step(g, p):
                    pool.wait_ge(transposed, done(g - 2))
                    normalize(nc, k, pool, xn[:, p, :], g, centered, normed)
                with pool.Fori(0, QUADS // 2) as t:
                    for u in (0, 1):
                        step(2 * t + u, u)

            @block.tensor
            def _(pe):
                for s in (transposed, m2_mm, m1_mm, t_turned, match_mm, selected, u_mm):
                    pe.sem_inc(s, BIAS)
                pe.wait_ge(consts, 32)

                def turn(g, p):
                    pe.wait_ge(normed, done(g))
                    pe.wait_ge(m1_copied, done(g - 1))
                    for i in range(G):
                        last = nc.tensor.transpose(psF[:, b(i)], xn[:, p, b(i)], k.ident[:, :])
                    last.then_inc(transposed, 1)

                def second(g, p):
                    pe.wait_ge(relued, done(g))
                    nc.tensor.matmul(psF[:, :], k.w2T[:, :], hT[:, p, :], start=True, stop=True).then_inc(m2_mm, 1)

                def first(g, p):
                    pe.wait_ge(m2_copied, done(g))
                    nc.tensor.matmul(psF[:, :], k.w1T[:, :], hT[:, p, :], start=True, stop=True).then_inc(m1_mm, 1)

                def prepare(g, i, r):
                    n = (g * G + i) * NG + r
                    chunks = range(4 * r, min(4 * r + 4, NCH))
                    if r == 0:
                        pe.wait_ge(tabled, done(g * G + i))
                    pe.wait_ge(tT_ready, done(n - 1))
                    for c in chunks:
                        last = nc.tensor.transpose(psTT[:, b(c % 4)],
                                                   table[:, i, 2 * c:2 * c + 2, :].rearrange("z q s -> z (q s)"), k.ident[:, :])
                    last.then_inc(t_turned, 1)
                    pe.wait_ge(onehot_ready, done(n - 1))
                    for c in chunks:
                        last = nc.tensor.matmul(psC[:, b(c % 4)], sel[:, c * 128:(c + 1) * 128],
                                                k.mask1[:, bass.ds((g * G + i) * N, N)], start=True, stop=True)
                    last.then_inc(match_mm, 1)

                def select(g, i, r):
                    n = (g * G + i) * NG + r
                    par = (i * NG + r) % 2
                    pe.wait_ge(tT_ready, done(n))
                    pe.wait_ge(onehot_ready, done(n))
                    pe.wait_ge(reduced, done(n - 2))
                    for c in range(4 * r, min(4 * r + 4, NCH)):
                        for q in (0, 1):
                            rows = slice(SUB * q, SUB * q + SUB)
                            last = nc.tensor.matmul(psS[:, 2 * par + q, b(c % 4)], tableT[rows, par, c % 4, :],
                                                    onehot[rows, par, c % 4, :], start=True, stop=True)
                    last.then_inc(selected, 1)

                def update(g, p):
                    pe.wait_ge(mT_ready, done(g))
                    pe.wait_ge(biased, done(g - 1))
                    for i in range(G):
                        nc.tensor.matmul(psU[:, b(i)], hT[:, p, b(i)], k.wuT[:, 0, :], start=True, stop=False)
                        last = nc.tensor.matmul(psU[:, b(i)], mT[:, p, b(i)], k.wuT[:, 1, :], start=False, stop=True)
                    last.then_inc(u_mm, 1)

                def quad(g, p, prev, next):
                    for at in range(ITEMS):
                        if at + 1 < ITEMS:
                            prepare(g, *divmod(at + 1, NG))
                        elif next:
                            prepare(g + 1, 0, 0)
                        select(g, *divmod(at, NG))
                        if at == NG - 1 and prev:
                            update(g - 1, 1 - p)
                        if at == NG - 1 and next:
                            turn(g + 1, 1 - p)
                        if at == NG and next:
                            second(g + 1, 1 - p)
                        if at == NG + 1 and next:
                            first(g + 1, 1 - p)
                turn(0, 0)
                second(0, 0)
                first(0, 0)
                prepare(0, 0, 0)
                quads(pe, quad)
                update(QUADS - 1, 1)

            @block.scalar
            def _(act):
                for s in (relued, m2_copied, m1_copied, tT_ready, onehot_ready, mT_ready):
                    act.sem_inc(s, BIAS)
                act.wait_ge(consts, 32)

                def relu(g, p):
                    act.wait_ge(transposed, done(g))
                    act.wait_ge(u_mm, done(g - 2))
                    nc.scalar.activation(hT[:, p, :], psF[:, :], ACT.Relu).then_inc(relued, 1)

                def second(g, p):
                    act.wait_ge(m2_mm, done(g))
                    act.wait_ge(tabled, done(g * G - (G + 1)))
                    act.wait_ge(padded, 1)
                    nc.scalar.activation(m2[:, p, :, 0:N], psF[:, :].rearrange("z (b n) -> z b n", n=N), ACT.Identity,
                                         bias=k.b2[:, 0:1]).then_inc(m2_copied, 1)

                def first(g, p):
                    act.wait_ge(m1_mm, done(g))
                    act.wait_ge(summed, done(g - 2))
                    nc.scalar.activation(m1[:, p, :], psF[:, :], ACT.Identity, bias=k.b1[:, 0:1]).then_inc(m1_copied, 1)

                def item(g, at):
                    n = g * ITEMS + at
                    w = min(4, NCH - 4 * (at % NG)) * N
                    flat = lambda t: t[:, at % 2, :, :].rearrange("r c n -> r (c n)")[:, 0:w]
                    act.wait_ge(t_turned, done(n))
                    act.wait_ge(selected, done(n - 2))
                    nc.scalar.activation(flat(tableT), psTT[:, 0:w], ACT.Copy).then_inc(tT_ready, 1)
                    act.wait_ge(match_mm, done(n))
                    nc.scalar.activation(flat(onehot), psC[:, 0:w], ACT.Relu, bias=nhot[:, 0:1]).then_inc(onehot_ready, 1)

                def update(g, p):
                    act.wait_ge(summed, done(g))
                    act.wait_ge(u_mm, done(g - 2))
                    nc.scalar.activation(mT[:, p, :], mx[:, :], ACT.Relu).then_inc(mT_ready, 1)

                def quad(g, p, prev, next):
                    for at in range(ITEMS):
                        item(g, at)
                        if at == 1 and prev:
                            update(g - 1, 1 - p)
                        if at == NG and next:
                            relu(g + 1, 1 - p)
                        if at == NG + 1 and next:
                            second(g + 1, 1 - p)
                        if at == NG + 2 and next:
                            first(g + 1, 1 - p)
                relu(0, 0)
                second(0, 0)
                first(0, 0)
                quads(act, quad)
                update(QUADS - 1, 1)

            @block.vector
            def _(dve):
                for s in (tabled, reduced, merged, summed, biased, added):
                    dve.sem_inc(s, BIAS)
                nc.vector.memset(table[:].rearrange("z b k s -> z (b k s)"), 0.0).then_inc(padded, 1)
                dve.wait_ge(padded, 1)
                nc.vector.memset(table[:, :, 0:NBLK, 0], LOWEST)
                nc.vector.memset(m2[:, :, :, N:PADN].rearrange("z p b j -> z (p b) j"), LOWEST).then_inc(padded, 1)
                dve.wait_ge(padded, 2)

                def tables(g, p, i, steps=range(BLK)):
                    n = g * G + i
                    if steps[0] == 0:
                        dve.wait_ge(m2_copied, done(g))
                        dve.wait_ge(t_turned, done(n * NG - ((G - 1) * NG + 1)))
                    node = m2[:, p, i, :].rearrange("z (k t) -> z k t", t=BLK)
                    for t in steps:
                        w = 2 ** t
                        if t > 0:
                            dve.wait_ge(grown, n * (BLK - 1) + t)
                        nc.vector.tensor_tensor(table[:, i, 0:NBLK, w:2 * w], table[:, i, 0:NBLK, 0:w],
                                                node[:, :, t:t + 1].broadcast_to([C, NBLK, w]),
                                                ALU.max).then_inc(grown if t < BLK - 1 else tabled, 1)

                def reduce(g, at):
                    n = g * ITEMS + at
                    i, r = divmod(at, NG)
                    w = min(4, NCH - 4 * r) * N
                    dve.wait_ge(selected, done(n))
                    dve.wait_ge(merged, done(g * G + (i - G)))
                    nc.vector.tensor_reduce(
                        part[:, i, r, :],
                        psS[:, 2 * (at % 2):2 * (at % 2) + 2, 0:w].rearrange("z q (c i) -> z i q c", i=N),
                        AX.XY, ALU.max).then_inc(reduced, 1)

                def merge(g, i):
                    dve.wait_ge(reduced, done(g * ITEMS + (i * NG + (NG - 1))))
                    dve.wait_ge(mT_ready, done(g - 1))
                    nc.vector.tensor_reduce(mx[:, b(i)], part[:, i, :, :].rearrange("z r i -> z i r"), AX.X,
                                            ALU.max).then_inc(merged, 1)

                def add_own(g, p):
                    dve.wait_ge(merged, done(g * G + (G - 1)))
                    nc.vector.tensor_tensor(mx[:, :], mx[:, :], m1[:, p, :], ALU.add).then_inc(summed, 1)

                def update(g):
                    dve.wait_ge(u_mm, done(g))
                    dve.wait_ge(added, done(g - 1))
                    nc.vector.tensor_tensor(
                        upd[:, :].rearrange("n (b c) -> n b c", c=C), psU[:, :].rearrange("n (b c) -> n b c", c=C),
                        k.bu[:, :].unsqueeze(1).broadcast_to([N, G, C]), ALU.add).then_inc(biased, 1)
                    dve.wait_ge(biased, done(g))
                    xs = k.x[:, bass.ds(g * QC, QC)]
                    nc.vector.scalar_tensor_tensor(out=xs, in0=upd[:, :], scalar=0.0, in1=xs, op0=ALU.max,
                                                   op1=ALU.add).then_inc(added, 1)

                def statistics(g):
                    dve.wait_ge(added, done(g))
                    ln_stats(nc, k, g)

                EARLY, LATE = range(BLK - 2), range(BLK - 2, BLK)

                def quad(g, p, prev, next):
                    def ahead(i, steps):
                        if next:
                            tables(g + 1, 1 - p, i, steps)
                    for at in range(ITEMS):
                        reduce(g, at)
                        if at % NG == NG - 1:
                            merge(g, at // NG)
                        if at == 0:
                            if prev:
                                add_own(g - 1, 1 - p)
                            tables(g, p, G - 1, EARLY)
                        if at == 1:
                            tables(g, p, G - 1, LATE)
                        if at == 3 and prev:
                            update(g - 1)
                        if at == 4 and prev:
                            statistics(g - 1)
                        if at >= 5 and at < 5 + 2 * (G - 1):
                            i, half = divmod(at - 5, 2)
                            ahead(i, LATE if half else EARLY)
                for i in range(G - 1):
                    tables(0, 0, i)
                quads(dve, quad)
                add_own(QUADS - 1, 1)
                update(QUADS - 1)
                statistics(QUADS - 1)


def phase_heads(nc, k):
    phase_norm(nc, k, "n2")
    with ExitStack() as ctx:
        sb = lambda name, shape, dt=F32: k.sb(ctx, "a_" + name, shape, dt)
        HC = HEADS * N
        KR = 32 + HEADS
        xn = sb("xn", [N, 2, QC])
        hT = sb("hT", [C, QC])
        hs = sb("h", [N, 2, QC])
        lhs = sb("lhs", [KR, 2, QC])
        s2 = sb("s2", [KR, 2, QC])
        ind = sb("ind", [KR, HC])
        rhs = sb("rhs", [KR, 2, HC])
        eu = sb("eu", [N, 2, HC])
        ex = sb("ex", [N, 2, HC])
        nmx = sb("nmx", [N, 2, HEADS])
        zs = sb("zs", [N, 2, HEADS])
        rz = sb("rz", [N, 2, HEADS])
        attT = sb("attT", [N, 2, N])
        psF, psA, psO = (k.ps(ctx, "a_" + n, [N, QC]) for n in ("psF", "psA", "psO"))
        psE = k.ps(ctx, "a_psE", [N, 2, HC])
        sem = lambda name: k.sem("a_" + name)
        consts, cleared, centered, normed, transposed, relued, h_mm, h_ready, s_mm, s_ready = (sem(n) for n in (
            "consts", "cleared", "centered", "normed", "transposed", "relued", "h_mm", "h_ready", "s_mm", "s_ready"))
        placed, e_mm, e_copied, leaky, negmax, expd = (sem(n) for n in (
            "placed", "e_mm", "e_copied", "leaky", "negmax", "expd"))
        recip, scaled, att_mm, att_ready, out_mm, added = (sem(n) for n in (
            "recip", "scaled", "att_mm", "att_ready", "out_mm", "added"))
        b = lambda i: slice(i * N, (i + 1) * N)

        def graphs(eng, slot):
            def quad(g, p, first=False, tail=False, left=2):
                for i in range(G):
                    slot(g, p, i, lambda lag: (not first or i >= lag) and (not tail or i < lag), lambda l: l <= left)
            quad(0, 0, first=True)
            with eng.Fori(0, QUADS // 2 - 2) as t:
                for u in (0, 1):
                    quad(2 * t + (u + 1), 1 - u)
            quad(QUADS - 3, 1)
            quad(QUADS - 2, 0, left=1)
            quad(QUADS - 1, 1, left=0)
            quad(QUADS, 0, tail=True, left=0)

        with nc.Block() as block:
            @block.sync
            def _(sp):
                sp.wait_ge(cleared, 1)
                sp.dma_start(ind[32:KR, :], k.a["c_blockind"]).then_inc(consts, 16)
                for p in (0, 1):
                    sp.dma_start(rhs[0:HEADS, p, :], k.a["c_blockind"]).then_inc(consts, 16)
                sp.wait_ge(consts, 48)

            @block.gpsimd
            def _(pool):
                for s in (centered, normed, placed):
                    pool.sem_inc(s, BIAS)
                pool.wait_ge(consts, 48)

                def center(g, p):
                    pool.wait_ge(transposed, done(g - 2))
                    normalize_center(nc, k, xn[:, p, :], g, centered)
                    pool.wait_ge(centered, done(g))

                def scale(g, p):
                    normalize_scale(nc, k, xn[:, p, :], g, normed)
                    pool.wait_ge(normed, done(g))

                def slot(g, p, i, behind, ahead):
                    n = g * G + i
                    if behind(0):
                        pool.wait_ge(s_ready, done(g))
                        pool.wait_ge(e_mm, done(n - 2))
                        nc.gpsimd.tensor_tensor(
                            rhs[32:KR, i % 2, :].rearrange("r (h j) -> r h j", j=N), ind[32:KR, :].rearrange("r (h j) -> r h j", j=N),
                            s2[32:KR, p, b(i)].unsqueeze(1).broadcast_to([HEADS, HEADS, N]), ALU.mult).then_inc(placed, 1)
                    if i in (1, 2) and ahead(2):
                        pool.wait_ge(placed, done(n))
                        (center if i == 1 else scale)(g + 2, p)
                for g in (0, 1):
                    center(g, g)
                    scale(g, g)
                graphs(pool, slot)

            @block.tensor
            def _(pe):
                for s in (transposed, h_mm, s_mm, e_mm, att_mm, out_mm):
                    pe.sem_inc(s, BIAS)
                pe.wait_ge(consts, 48)

                def turn(g, p):
                    pe.wait_ge(normed, done(g))
                    pe.wait_ge(h_ready, done(g - 1))
                    for i in range(G):
                        last = nc.tensor.transpose(psF[:, b(i)], xn[:, p, b(i)], k.ident[:, :])
                    last.then_inc(transposed, 1)

                def node_scores(g):
                    pe.wait_ge(relued, done(g))
                    nc.tensor.matmul(psF[0:HEADS, :], k.wa[:, 0, :], hT[:, :], start=True, stop=True)
                    nc.tensor.matmul(psF[32:KR, :], k.wa[:, 1, :], hT[:, :], start=True, stop=True).then_inc(s_mm, 1)

                def hidden(g):
                    pe.wait_ge(s_ready, done(g))
                    for i in range(G):
                        last = nc.tensor.matmul(psF[:, b(i)], hT[:, b(i)], k.wl2[:, :], start=True, stop=True)
                    last.then_inc(h_mm, 1)

                def slot(g, p, i, behind, ahead):
                    n = g * G + i
                    if behind(0):
                        pe.wait_ge(s_ready, done(g))
                        pe.wait_ge(placed, done(n))
                        pe.wait_ge(e_copied, done(n - 2))
                        for half in (0, 1):
                            at = psE[:, i % 2, half * 512:(half + 1) * 512]
                            nc.tensor.matmul(at, lhs[:, p, b(i)], rhs[:, i % 2, half * 512:(half + 1) * 512], start=True, stop=False)
                            last = nc.tensor.matmul(at.rearrange("n (h j) -> n h j", j=N), k.identb[:, :],
                                                    k.negm[:, bass.ds(n * N, N)].unsqueeze(1).broadcast_to([N, 4, N]),
                                                    start=False, stop=True)
                        last.then_inc(e_mm, 1)
                    if behind(4):
                        pe.wait_ge(att_ready, done(n - 4))
                        if i == 0:
                            pe.wait_ge(added, done(g - 2))
                        nc.tensor.matmul(psO[:, b(i)], attT[:, i % 2, :], hs[:, 1 - p, b(i)], start=True, stop=True).then_inc(out_mm, 1)
                    if i == 1 and ahead(1):
                        turn(g + 1, 1 - p)
                    if i == 2 and ahead(1):
                        node_scores(g + 1)
                    if i == 3 and ahead(1):
                        hidden(g + 1)
                    if behind(3):
                        m = n - 3
                        pe.wait_ge(scaled, done(m))
                        pe.wait_ge(att_ready, done(m - 1))
                        for h in range(HEADS):
                            last = nc.tensor.matmul(psA[:, 0:N], ex[:, (i - 3) % 2, b(h)], k.ident[:, :],
                                                    start=h == 0, stop=h == HEADS - 1)
                        last.then_inc(att_mm, 1)
                turn(0, 0)
                node_scores(0)
                hidden(0)
                graphs(pe, slot)

            @block.scalar
            def _(act):
                for s in (relued, h_ready, e_copied, expd):
                    act.sem_inc(s, BIAS)

                def relu(g):
                    act.wait_ge(transposed, done(g))
                    act.wait_ge(h_mm, done(g - 1))
                    nc.scalar.activation(hT[:, :], psF[:, :], ACT.Relu).then_inc(relued, 1)

                def hidden(g, p):
                    act.wait_ge(h_mm, done(g))
                    act.wait_ge(out_mm, done(G * g - (G + 1)))
                    nc.scalar.activation(hs[:, p, :], psF[:, :], ACT.Copy).then_inc(h_ready, 1)

                def slot(g, p, i, behind, ahead):
                    n = g * G + i
                    if behind(2):
                        m = n - 2
                        act.wait_ge(negmax, done(m))
                        act.wait_ge(att_mm, done(m - 2))
                        act.wait_ge(recip, done(m - 2))
                        for h in range(HEADS):
                            last = nc.scalar.activation(ex[:, i % 2, b(h)], eu[:, i % 2, b(h)], ACT.Exp,
                                                        bias=nmx[:, i % 2, h:h + 1], accum_out=zs[:, i % 2, h:h + 1])
                        last.then_inc(expd, 1)
                    if behind(0):
                        act.wait_ge(e_mm, done(n))
                        act.wait_ge(expd, done(n - 2))
                        nc.scalar.activation(eu[:, i % 2, :], psE[:, i % 2, :], ACT.Copy).then_inc(e_copied, 1)
                    if i == 1 and ahead(1):
                        relu(g + 1)
                    if i == 3 and ahead(1):
                        hidden(g + 1, 1 - p)
                relu(0)
                hidden(0, 0)
                graphs(act, slot)

            @block.vector
            def _(dve):
                for s in (s_ready, leaky, negmax, recip, scaled, att_ready, added):
                    dve.sem_inc(s, BIAS)
                nc.vector.memset(lhs[:].rearrange("r p c -> r (p c)"), 0.0)
                nc.vector.memset(rhs[:].rearrange("r p c -> r (p c)"), 0.0).then_inc(cleared, 1)
                dve.wait_ge(cleared, 1)
                nc.vector.memset(lhs[32:KR, :, :].rearrange("r p c -> r (p c)"), 1.0)

                def node_scores(g, p):
                    dve.wait_ge(s_mm, done(g))
                    dve.wait_ge(e_mm, done(G * g - (G + 1)))
                    nc.vector.tensor_scalar(lhs[0:HEADS, p, :], psF[0:HEADS, :], k.ab[:, 0:1], None, ALU.add)
                    nc.vector.tensor_copy(s2[32:KR, p, :], psF[32:KR, :]).then_inc(s_ready, 1)

                def finish(g):
                    dve.wait_ge(out_mm, done(g * G + (G - 1)))
                    xs = k.x[:, bass.ds(g * QC, QC)]
                    nc.vector.tensor_tensor(xs, psO[:, :], xs, ALU.add).then_inc(added, 1)
                    dve.wait_ge(added, done(g))
                    ln_stats(nc, k, g)

                def slot(g, p, i, behind, ahead):
                    n = g * G + i
                    odd, even = (i - 1) % 2, i % 2
                    if behind(3):
                        m = n - 3
                        dve.wait_ge(expd, done(m))
                        dve.wait_ge(scaled, done(m - 2))
                        nc.vector.reciprocal(rz[:, odd, :], zs[:, odd, :]).then_inc(recip, 1)
                        dve.wait_ge(recip, done(m))
                        per_head = ex[:, odd, :].rearrange("n (h j) -> n h j", j=N)
                        nc.vector.tensor_tensor(per_head, per_head, rz[:, odd, :].unsqueeze(2).broadcast_to([N, HEADS, N]),
                                                ALU.mult).then_inc(scaled, 1)
                    if behind(4):
                        m = n - 4
                        dve.wait_ge(att_mm, done(m))
                        dve.wait_ge(out_mm, done(m - 2))
                        nc.vector.tensor_scalar(attT[:, even, :], psA[:, 0:N], 1.0 / HEADS, None, ALU.mult).then_inc(att_ready, 1)
                    if behind(1):
                        m = n - 1
                        dve.wait_ge(e_copied, done(m))
                        nc.vector.scalar_tensor_tensor(out=eu[:, odd, :], in0=eu[:, odd, :], scalar=0.01, in1=eu[:, odd, :],
                                                       op0=ALU.mult, op1=ALU.max).then_inc(leaky, 1)
                        dve.wait_ge(leaky, done(m))
                        dve.wait_ge(expd, done(m - 2))
                        nc.vector.tensor_reduce(nmx[:, odd, :], eu[:, odd, :].rearrange("n (h j) -> n h j", j=N), AX.X, ALU.max,
                                                negate=True).then_inc(negmax, 1)
                    if i == 2 and ahead(1):
                        node_scores(g + 1, 1 - p)
                    if i == 3 and behind(4):
                        finish(g - 1)
                node_scores(0, 0)
                graphs(dve, slot)


DUP = N + HID
SLABS = 4
DS = 8
HALF = DS * N
SC = 2 * HALF


def phase_pairs(nc, k, a, out):
    phase_norm(nc, k, "n3")
    with ExitStack() as ctx:
        hd = k.sb(ctx, "hd", [C, B * DUP], F32)
        hy = k.sb(ctx, "hy", [N, B * C], F32)
        alpha = k.sb(ctx, "p_alpha", [N, 1], F32)
        beta = k.sb(ctx, "p_beta", [N, 1], F32)
        diag0 = k.sb(ctx, "p_diag0", [N, 2 * N], F32)
        ystats = k.sb(ctx, "y_stats", [C, B, 6], F32)
        scratch = nc.dram_tensor("pair_scores", (2, N * 2 * N), F32).ap()
        phase_pair_inputs(nc, k, hd, hy)
        with ExitStack() as dctx:
            dif = k.sb(dctx, "p_dif", [C, 2, SC], F32)
            phase_pair_stats(nc, k, hd, dif, alpha, beta, diag0)
            phase_pair_scores(nc, k, hd, hy, dif, alpha, beta, diag0, scratch, ystats)
        phase_output(nc, k, hd, hy, ystats, out)


def phase_pair_inputs(nc, k, hd, hy):
    with ExitStack() as ctx:
        xn = k.sb(ctx, "i_xn", [N, 2, QC], F32)
        hT = k.sb(ctx, "i_hT", [C, 2, QC], F32)
        psT, psH = k.ps(ctx, "i_psT", [N, QC]), k.ps(ctx, "i_psH", [N, QC])
        sem = lambda name: k.sem("i_" + name)
        centered, normed, transposed, relued, copied, h_mm, h_ready = (sem(n) for n in (
            "centered", "normed", "transposed", "relued", "copied", "h_mm", "h_ready"))
        b = lambda i: slice(i * N, (i + 1) * N)

        def quads(eng, step):
            with eng.Fori(0, QUADS // 2) as t:
                for u in (0, 1):
                    step(2 * t + u, u)

        with nc.Block() as block:
            @block.gpsimd
            def _(pool):
                for s in (centered, normed):
                    pool.sem_inc(s, BIAS)

                def step(g, p):
                    pool.wait_ge(transposed, done(g - 2))
                    normalize(nc, k, pool, xn[:, p, :], g, centered, normed)
                quads(pool, step)

            @block.tensor
            def _(pe):
                for s in (transposed, h_mm):
                    pe.sem_inc(s, BIAS)

                def step(g, p):
                    pe.wait_ge(normed, done(g))
                    pe.wait_ge(relued, done(g - 1))
                    for i in range(G):
                        last = nc.tensor.transpose(psT[:, b(i)], xn[:, p, b(i)], k.ident[:, :])
                    last.then_inc(transposed, 1)
                    pe.wait_ge(relued, done(g))
                    pe.wait_ge(h_ready, done(g - 1))
                    for i in range(G):
                        last = nc.tensor.matmul(psH[:, b(i)], hT[:, p, b(i)], k.wgT[:, :], start=True, stop=True)
                    last.then_inc(h_mm, 1)
                quads(pe, step)

            @block.scalar
            def _(act):
                for s in (relued, h_ready):
                    act.sem_inc(s, BIAS)

                def step(g, p):
                    act.wait_ge(transposed, done(g))
                    act.wait_ge(h_mm, done(g - 2))
                    act.wait_ge(copied, done(g - 2))
                    nc.scalar.activation(hT[:, p, :], psT[:, :], ACT.Relu).then_inc(relued, 1)
                    act.wait_ge(h_mm, done(g))
                    nc.scalar.activation(hy[:, bass.ds(g * QC, QC)], psH[:, :], ACT.Copy).then_inc(h_ready, 1)
                quads(act, step)

            @block.vector
            def _(dve):
                dve.sem_inc(copied, BIAS)

                def step(g, p):
                    dve.wait_ge(relued, done(g))
                    src = hT[:, p, :].rearrange("c (b n) -> c b n", n=N)
                    dst = hd[:, bass.ds(g * (G * DUP), G * DUP)].rearrange("c (b n) -> c b n", n=DUP)
                    nc.vector.tensor_copy(dst[:, :, 0:N], src)
                    nc.vector.tensor_copy(dst[:, :, N:DUP], src[:, :, 0:HID]).then_inc(copied, 1)
                quads(dve, step)


def windows(hd, n, s):
    one = hd[:, bass.ds(n * DUP, N)]
    far = hd[:, bass.ds(n * DUP + (1 + DS * s), N)]
    part = list(one.ap)[0]
    return (bass.AP(one.tensor, one.offset, [part, [0, 2], [0, DS], [1, N]]),
            bass.AP(far.tensor, far.offset, [part, [HID // 2, 2], [1, DS], [1, N]]))


def phase_pair_stats(nc, k, hd, dif, alpha, beta, diag0):
    with ExitStack() as ctx:
        sb = lambda name, shape, dt=F32: k.sb(ctx, "v_" + name, shape, dt)
        D = sb("abs", [C, 3, SC])
        place = lambda s: 2 if s == SLABS - 1 else s % 2
        before = lambda m, s: m - 2 if s in (0, 2) else m - SLABS
        dif3 = sb("dif3", [C, SC])
        difs = lambda buf, cols=slice(0, SC): dif3[:, cols] if buf == 2 else dif[:, buf, cols]
        dsum = sb("dsum", [C, B * SLABS])
        hsq = sb("hsq", [N, B * SLABS])
        junk = sb("junk", [N, 2, HALF])
        dsumv = sb("dsumv", [C, B])
        tot = sb("tot", [N, 3])
        fold = sb("fold", [N, N])
        ones = sb("ones", [N, N])
        v = sb("v", [N, 12])
        psW = k.ps(ctx, "v_psW", [N, 3, HALF])
        psS = k.ps(ctx, "v_psS", [N, 512])
        sem = lambda name: k.sem("v_" + name)
        cleared, consts, sub_done, vabs_done, abs_done, w_mm, squared, totals, folded, algebra, rooted, own_mm = (sem(n) for n in (
            "cleared", "consts", "sub_done", "vabs_done", "abs_done", "w_mm", "squared", "totals", "folded", "algebra", "rooted", "own_mm"))
        PAIRS = float(B * N * N)

        VCOLS = 1280

        def graphs(eng, step):
            step(0, 0, True)
            with eng.Fori(0, (B - 1) // 3) as t:
                for u in range(3):
                    step(3 * t + (u + 1), SLABS * (u + 1) % 3, False)

        with nc.Block() as block:
            @block.sync
            def _(sp):
                sp.dma_start(fold[:, :], k.a["c_fold"]).then_inc(consts, 16)
                sp.wait_ge(consts, 16)

            @block.vector
            def _(dve):
                for s in (sub_done, vabs_done):
                    dve.sem_inc(s, BIAS)
                nc.vector.memset(D[:, place(SLABS - 1), SC - HID:SC], 0.0)
                nc.vector.memset(ones[:, :], 1.0).then_inc(cleared, 1)

                def step(n, buf0, first):
                    for s in range(SLABS):
                        m = n * SLABS + s
                        buf = (buf0 + s) % 3
                        dve.wait_ge(abs_done, done(m - 3))
                        if s == 2:
                            dve.wait_ge(vabs_done, done(n - 1))
                        one, far = windows(hd, n, s)
                        nc.vector.tensor_tensor(difs(buf).rearrange("c (h d i) -> c h d i", h=2, i=N), one, far,
                                                ALU.subtract).then_inc(sub_done, 1)
                    dve.wait_ge(sub_done, done(m))
                    dve.wait_ge(w_mm, done(m - SLABS))
                    nc.vector.scalar_tensor_tensor(
                        out=D[:, place(SLABS - 1), 0:VCOLS], in0=difs(buf, slice(0, VCOLS)), scalar=-1.0, in1=difs(buf, slice(0, VCOLS)),
                        op0=ALU.mult, op1=ALU.max, accum_out=dsumv[:, bass.ds(n, 1)]).then_inc(vabs_done, 1)
                graphs(dve, step)

                dve.wait_ge(squared, done(B * SLABS - 1))
                dve.wait_ge(vabs_done, done(B - 1))
                nc.vector.tensor_reduce(tot[:, 0:1], dsum[:, :], AX.X, ALU.add)
                nc.vector.tensor_reduce(tot[:, 2:3], dsumv[:, :], AX.X, ALU.add)
                nc.vector.tensor_reduce(tot[:, 1:2], hsq[:, :], AX.X, ALU.add).then_inc(totals, 1)
                at = [0]

                def link(ins):
                    at[0] += 1
                    ins.then_inc(algebra, 1)
                    dve.wait_ge(algebra, at[0])
                c = lambda i: v[:, i:i + 1]
                b1, g1, be1, w2, b2 = (k.pcol[:, i:i + 1] for i in range(5))
                dve.wait_ge(folded, 1)
                link(nc.vector.tensor_scalar(c(0), psS[:, 0:1], 2.0 / PAIRS, None, ALU.mult))
                link(nc.vector.tensor_scalar(c(1), psS[:, 1:2], 2.0 / PAIRS, None, ALU.mult))
                link(nc.vector.tensor_tensor(c(2), c(0), c(0), ALU.mult))
                link(nc.vector.tensor_tensor(c(3), c(1), c(2), ALU.subtract))
                link(nc.vector.tensor_scalar(c(4), c(3), EPS, None, ALU.add))
                dve.wait_ge(rooted, 1)
                link(nc.vector.reciprocal(c(6), c(5)))
                link(nc.vector.tensor_tensor(alpha[:, :], c(6), g1, ALU.mult))
                link(nc.vector.tensor_tensor(c(7), c(0), b1, ALU.add))
                link(nc.vector.tensor_tensor(c(7), b1, c(7), ALU.subtract))
                link(nc.vector.scalar_tensor_tensor(out=beta[:, :], in0=c(7), scalar=alpha[:, 0:1], in1=be1,
                                                    op0=ALU.mult, op1=ALU.add))
                link(nc.vector.scalar_tensor_tensor(out=c(8), in0=beta[:, :], scalar=0.01, in1=beta[:, :],
                                                    op0=ALU.mult, op1=ALU.max))
                link(nc.vector.tensor_tensor(c(9), c(8), w2, ALU.mult))
                link(nc.vector.tensor_scalar(junk[:, 0, 0:N], ones[:, :], c(9), None, ALU.mult))
                dve.wait_ge(own_mm, 1)
                link(nc.vector.tensor_tensor(c(10), psS[:, 4:5], b2, ALU.add))
                link(nc.vector.memset(diag0[:, :], 0.0))
                link(nc.vector.tensor_scalar(diag0[:, 0:N], k.ident[:, :], c(10), 0.5, ALU.mult, ALU.mult))

            @block.scalar
            def _(act):
                for s in (abs_done, squared):
                    act.sem_inc(s, BIAS)
                act.wait_ge(cleared, 1)

                def absolute(n, s, buf):
                    m = n * SLABS + s
                    cols = slice(VCOLS, SC - HID) if s == SLABS - 1 else slice(0, SC)
                    act.wait_ge(sub_done, done(m))
                    act.wait_ge(w_mm, done(before(m, s)))
                    nc.scalar.activation(D[:, place(s), cols], difs(buf, cols), ACT.Abs,
                                         accum_out=dsum[:, bass.ds(m, 1)]).then_inc(abs_done, 1)

                def square(m, s, buf):
                    act.wait_ge(w_mm, done(m))
                    act.wait_ge(squared, done(m - 2))
                    nc.scalar.activation(junk[:, s % 2, :], psW[:, buf, :], ACT.Square,
                                         accum_out=hsq[:, bass.ds(m, 1)]).then_inc(squared, 1)

                def step(n, buf0, first):
                    for s in range(SLABS):
                        absolute(n, s, (buf0 + s) % 3)
                        if s >= 2 or not first:
                            square(n * SLABS + (s - 2), s, (buf0 + s + 1) % 3)
                graphs(act, step)
                for s in (2, 3):
                    square((B - 1) * SLABS + s, s, ((B - 1) * SLABS + s) % 3)
                act.wait_ge(algebra, 5)
                nc.scalar.activation(v[:, 5:6], v[:, 4:5], ACT.Sqrt).then_inc(rooted, 1)

            @block.tensor
            def _(pe):
                pe.sem_inc(w_mm, BIAS)
                pe.wait_ge(consts, 16)
                pe.wait_ge(cleared, 1)

                def step(n, buf0, first):
                    for s in range(SLABS):
                        m = n * SLABS + s
                        buf = (buf0 + s) % 3
                        pe.wait_ge(abs_done, done(m))
                        if s == SLABS - 1:
                            pe.wait_ge(vabs_done, done(n))
                        pe.wait_ge(squared, done(m - 3))
                        last = pair_product(nc, k, psW[:, buf, :], D[:, place(s), :])
                        last.then_inc(w_mm, 1)
                graphs(pe, step)
                pe.wait_ge(totals, 1)
                for half in (0, HID):
                    for part in (0, 2):
                        nc.tensor.matmul(psS[half:half + HID, 0:1], k.p1T[:, :], tot[:, part:part + 1], start=part == 0,
                                         stop=part == 2)
                nc.tensor.matmul(psS[:, 1:2], fold[:, :], tot[:, 1:2], start=True, stop=True).then_inc(folded, 1)
                pe.wait_ge(algebra, 13)
                nc.tensor.matmul(psS[:, 4:5], junk[0:HID, 0, 0:N], ones[0:HID, 0:1], start=True, stop=True).then_inc(own_mm, 1)


def pair_product(nc, k, ps, D):
    for c in range(0, HALF, 512):
        nc.tensor.matmul(ps[0:HID, c:c + 512], k.p1T[:, :], D[:, c:c + 512], start=True, stop=True)
        last = nc.tensor.matmul(ps[HID:N, c:c + 512], k.p1T[:, :], D[:, HALF + c:HALF + c + 512], start=True, stop=True)
    return last


def phase_pair_scores(nc, k, hd, hy, dif, alpha, beta, diag0, scratch, ystats):
    with ExitStack() as ctx:
        sb = lambda name, shape, dt=F32: k.sb(ctx, "s_" + name, shape, dt)
        D = sb("abs", [C, 2, SC])
        place = sb("place", [N, 2, 32])
        LINEAR = (2, 3)
        linear = sb("linear", [C, 2, 32])
        w1 = sb("w1", [HID, C])
        coef = sb("coef", [N, 2])
        linrows = sb("linrows", [N, 1])
        linshare = sb("linshare", [N, 1])
        rowbias = sb("rowbias", [N, 1])
        dmask = sb("dmask", [N, HID])
        hid = sb("hid", [N, SLABS, HALF])
        rows = sb("rows", [N, 512])
        rot = sb("rot", [N, 2, HID])
        wide = sb("wide", [N, 2, 2 * N])
        fwd = sb("fwd", [N, 2, N])
        nmx = sb("nmx", [N, 2])
        zs = sb("zs", [N, 2])
        rz = sb("rz", [N, 2])
        ex = sb("ex", [N, 2, N])
        dg = sb("dg", [N, 2, N])
        attT = sb("attT", [N, 2, N])
        hg = sb("hg", [N, 2, C])
        psW = k.ps(ctx, "s_psW", [N, 2, HALF])
        psR, psT, psM, psA = (k.ps(ctx, "s_" + n, [N, 512]) for n in ("psR", "psT", "psM", "psA"))
        sem = lambda name: k.sem("s_" + name)
        consts, cleared, set_up, unfolded, lin_mm, prefilled, sub_done, abs_done, w_mm, h_copied, hid_done, r_mm = (sem(n) for n in (
            "consts", "cleared", "set_up", "unfolded", "lin_mm", "prefilled", "sub_done", "abs_done", "w_mm", "h_copied", "hid_done", "r_mm"))
        rows_ready, turned, rot_ready, written, back, fwd_ready, m_mm, negmax, expd = (sem(n) for n in (
            "rows_ready", "turned", "rot_ready", "written", "back", "fwd_ready", "m_mm", "negmax", "expd"))
        recip, dg_ready, att_mm, att_ready, hg_ready, y_mm, y_ready, counted = (sem(n) for n in (
            "recip", "dg_ready", "att_mm", "att_ready", "hg_ready", "y_mm", "y_ready", "counted"))

        def graphs(eng, step):
            def peeled(n):
                step(n, n % 2, *(0 <= n - lag < B for lag in range(6)))
            for n in range(6):
                peeled(n)
            with eng.Fori(0, (B - 6) // 2) as t:
                for u in (0, 1):
                    step(2 * t + (u + 6), u, *(True for lag in range(6)))
            for n in range(B, B + 5):
                peeled(n)

        def behind(n, s, lag, zero, one):
            if s >= lag:
                return (n * SLABS + (s - lag), s - lag, n) if zero else None
            return (n * SLABS + (s - lag), s - lag + SLABS, n - 1) if one else None

        with nc.Block() as block:
            @block.sync
            def _(sp):
                sp.dma_start(dmask[:, :], k.a["c_dmask"]).then_inc(consts, 16)
                sp.dma_start(w1[:, :], k.a["L3_gnn_W1"]).then_inc(consts, 16)
                sp.dma_start(linrows[:, :], k.a["c_linrows"]).then_inc(consts, 16)
                for p in (0, 1):
                    sp.dma_start(scratch[p].rearrange("(i j) -> i j", j=2 * N), diag0[:, :]).then_inc(prefilled, 16)
                sp.wait_ge(consts, 48)
                sp.wait_ge(prefilled, 32)

                def step(n, p, zero, one, two, three, four, five):
                    if not two:
                        return
                    m = n - 2
                    sp.wait_ge(rot_ready, done(m))
                    dst = scratch[p]
                    sp.dma_start(bass.AP(dst.tensor, dst.offset + 1, [[2 * N + 1, N], [1, HID]]), rot[:, p, :]).then_inc(written, 16)
                    sp.wait_ge(written, 16 * (n - 1))
                    sp.dma_start(wide[:, p, :], dst.rearrange("(i j) -> i j", j=2 * N)).then_inc(back, 16)
                graphs(sp, step)

            @block.gpsimd
            def _(pool):
                pool.sem_inc(hg_ready, BIAS)

                def step(n, p, zero, one, two, three, four, five):
                    if two:
                        m = n - 2
                        pool.wait_ge(y_mm, done(m - 2))
                        nc.gpsimd.tensor_copy(hg[:, p, :], hy[:, bass.ds(m * C, C)]).then_inc(hg_ready, 1)
                graphs(pool, step)

            @block.vector
            def _(dve):
                for s in (sub_done, hid_done, rot_ready, fwd_ready, negmax, recip, dg_ready, att_ready, counted):
                    dve.sem_inc(s, BIAS)
                w2 = k.pcol[:, 3:4]
                nc.vector.memset(linear[:].rearrange("r m c -> r (m c)"), 0.0)
                nc.vector.memset(dg[:].rearrange("r p c -> r (p c)"), 1.0)
                nc.vector.tensor_tensor(coef[:, 0:1], alpha[:, :], w2, ALU.mult)
                nc.vector.tensor_tensor(coef[:, 1:2], beta[:, :], w2, ALU.mult)
                nc.vector.memset(place[:].rearrange("r m c -> r (m c)"), 0.0).then_inc(cleared, 1)
                dve.wait_ge(cleared, 1)
                for m, share in ((0, 1.0), (1, 0.99)):
                    nc.vector.tensor_scalar(place[0:HID, m, m:m + 1], k.pcol[0:HID, 3:4], share, None, ALU.mult)
                    nc.vector.tensor_scalar(place[HID:N, m, 2 + m:3 + m], k.pcol[HID:N, 3:4], share, None, ALU.mult)
                nc.vector.tensor_scalar(dg[:, 0, :], dg[:, 0, :], coef[:, 1:2], None, ALU.mult).then_inc(set_up, 1)
                dve.wait_ge(consts, 48)
                nc.vector.tensor_scalar(linshare[:, :], linrows[:, :], 0.01, None, ALU.mult).then_inc(set_up, 1)
                dve.wait_ge(unfolded, 1)
                dve.wait_ge(set_up, 2)
                for half in (0, 1):
                    nc.vector.tensor_scalar(linear[:, half, 2 * half + 1:2 * half + 2], psA[:, 0:1], 0.01, None, ALU.mult)
                nc.vector.scalar_tensor_tensor(out=rowbias[:, :], in0=psA[:, 1:2], scalar=linshare[:, 0:1], in1=k.pcol[:, 4:5],
                                               op0=ALU.mult, op1=ALU.add).then_inc(set_up, 1)

                def subtract(n, s):
                    m = n * SLABS + s
                    dve.wait_ge(abs_done, done(m - 2))
                    one, far = windows(hd, n, s)
                    nc.vector.tensor_tensor(dif[:, s % 2, :].rearrange("c (h d i) -> c h d i", h=2, i=N), one, far,
                                            ALU.subtract).then_inc(sub_done, 1)

                def leaky(m, s, n):
                    dve.wait_ge(h_copied, done(m))
                    nc.vector.scalar_tensor_tensor(out=hid[:, s, :], in0=hid[:, s, :], scalar=0.01, in1=hid[:, s, :],
                                                   op0=ALU.mult, op1=ALU.max).then_inc(hid_done, 1)

                def step(n, p, zero, one, two, three, four, five):
                    q = 1 - p
                    for s in range(SLABS):
                        if zero:
                            subtract(n, s)
                        late = behind(n, s, 3, zero, one)
                        if late and late[1] not in LINEAR:
                            leaky(*late)
                        if s == 1 and two:
                            m = n - 2
                            dve.wait_ge(turned, done(m))
                            if three:
                                dve.wait_ge(written, 16 * (n - 3))
                            dve.wait_ge(fwd_ready, done(m - 2))
                            nc.vector.tensor_tensor(
                                rot[:, p, :].rearrange("i (s q d) -> i s q d", s=4, q=4),
                                psT[:, :].rearrange("i (d q s) -> i s q d", d=4, q=4)[:, 0:4],
                                dmask[:, :].rearrange("i (s q d) -> i s q d", s=4, q=4), ALU.mult).then_inc(rot_ready, 1)
                        if s == 3 and two:
                            m = n - 2
                            dve.wait_ge(back, 16 * (n - 1))
                            dve.wait_ge(m_mm, done(m - 2))
                            nc.vector.tensor_tensor(fwd[:, p, :], wide[:, p, 0:N], wide[:, p, N:2 * N], ALU.add).then_inc(fwd_ready, 1)
                        if s == 2 and three:
                            m = n - 3
                            dve.wait_ge(m_mm, done(m))
                            dve.wait_ge(expd, done(m - 2))
                            nc.vector.tensor_reduce(nmx[:, q:q + 1], psM[:, 0:N], AX.X, ALU.max, negate=True).then_inc(negmax, 1)
                        if s == 0 and four:
                            m = n - 4
                            dve.wait_ge(expd, done(m))
                            dve.wait_ge(dg_ready, done(m - 2))
                            nc.vector.reciprocal(rz[:, p:p + 1], zs[:, p:p + 1]).then_inc(recip, 1)
                            dve.wait_ge(recip, done(m))
                            dve.wait_ge(att_mm, done(m - 2))
                            nc.vector.tensor_scalar(dg[:, p, :], k.ident[:, :], rz[:, p:p + 1], None, ALU.mult).then_inc(dg_ready, 1)
                        if s == 2 and four:
                            m = n - 4
                            dve.wait_ge(att_mm, done(m))
                            dve.wait_ge(y_mm, done(m - 2))
                            nc.vector.tensor_copy(attT[:, p, :], psA[:, 0:N]).then_inc(att_ready, 1)
                        if s == 1 and five:
                            m = n - 5
                            dve.wait_ge(y_ready, done(m))
                            nc.vector.bn_stats(ystats[:, bass.ds(m, 1), :], hy[:, bass.ds(m * C, C)]).then_inc(counted, 1)
                graphs(dve, step)

            @block.scalar
            def _(act):
                for s in (abs_done, h_copied, rows_ready, expd, y_ready):
                    act.sem_inc(s, BIAS)
                act.wait_ge(set_up, 3)

                def absolute(n, s):
                    m = n * SLABS + s
                    act.wait_ge(sub_done, done(m))
                    act.wait_ge(w_mm, done(m - 2))
                    if s < 2:
                        act.wait_ge(lin_mm, done(2 * n - 2 + s))
                    nc.scalar.activation(D[:, s % 2, :], dif[:, s % 2, :], ACT.Abs).then_inc(abs_done, 1)

                def hidden(m, s):
                    act.wait_ge(w_mm, done(m))
                    act.wait_ge(r_mm, done(m - SLABS))
                    nc.scalar.activation(hid[:, s, :], psW[:, s % 2, :], ACT.Relu if s in LINEAR else ACT.Identity, bias=beta[:, 0:1],
                                         scale=alpha[:, 0:1]).then_inc(h_copied, 1)

                def step(n, p, zero, one, two, three, four, five):
                    q = 1 - p
                    for s in range(SLABS):
                        if zero:
                            absolute(n, s)
                        if s == 2 and one:
                            m = n - 1
                            act.wait_ge(r_mm, done(SLABS * n - 1))
                            act.wait_ge(turned, done(m - 1))
                            nc.scalar.activation(rows[:, :], psR[:, :], ACT.Identity, bias=rowbias[:, 0:1]).then_inc(rows_ready, 1)
                        late = behind(n, s, 1, zero, one)
                        if late:
                            hidden(*late[0:2])
                        if s == 3 and three:
                            m = n - 3
                            act.wait_ge(negmax, done(m))
                            act.wait_ge(att_mm, done(m - 2))
                            act.wait_ge(recip, done(m - 2))
                            nc.scalar.activation(ex[:, q, :], psM[:, 0:N], ACT.Exp, bias=nmx[:, q:q + 1],
                                                 accum_out=zs[:, q:q + 1]).then_inc(expd, 1)
                        if s == 0 and five:
                            m = n - 5
                            act.wait_ge(y_mm, done(m))
                            act.wait_ge(hg_ready, done(m))
                            nc.scalar.activation(hy[:, bass.ds(m * C, C)], psA[:, 128:256], ACT.Identity,
                                                 bias=k.pcol[:, 5:6]).then_inc(y_ready, 1)
                graphs(act, step)

            @block.tensor
            def _(pe):
                for s in (w_mm, lin_mm, r_mm, turned, m_mm, att_mm, y_mm):
                    pe.sem_inc(s, BIAS)
                pe.wait_ge(consts, 48)
                pe.wait_ge(set_up, 1)
                nc.tensor.matmul(psA[:, 0:1], w1[:, :], coef[0:HID, 0:1], start=True, stop=True)
                nc.tensor.matmul(psA[:, 1:2], dg[0:HID, 0, :], dg[0:HID, 1, 0:1], start=True, stop=True).then_inc(unfolded, 1)
                pe.wait_ge(set_up, 3)

                def product(n, s):
                    m = n * SLABS + s
                    pe.wait_ge(abs_done, done(m))
                    pe.wait_ge(h_copied, done(m - 2))
                    pair_product(nc, k, psW[:, s % 2, :], D[:, s % 2, :]).then_inc(w_mm, 1)

                def second(m, s, n):
                    if s in LINEAR:
                        pe.wait_ge(h_copied, done(m))
                    else:
                        pe.wait_ge(hid_done, done(2 * n + s))
                    for c in (0, 1):
                        at, q = divmod(2 * s + c, 4)
                        last = nc.tensor.matmul(psR[32 * q:32 * q + 32, :], place[:, at, :], hid[:, s, c * 512:(c + 1) * 512],
                                                start=False, stop=at == 1)
                    last.then_inc(r_mm, 1)

                def linear_part(n, s):
                    pe.wait_ge(rows_ready, done(n - 1))
                    for c in (0, 1):
                        at, q = divmod(2 * s + c, 4)
                        for half in (0, 1):
                            col = half * HALF + c * 512
                            last = nc.tensor.matmul(psR[32 * q:32 * q + 32, :], linear[:, half, :], D[:, s % 2, col:col + 512],
                                                    start=half == 0, stop=False)
                    last.then_inc(lin_mm, 1)

                def step(n, p, zero, one, two, three, four, five):
                    q = 1 - p
                    for s in range(SLABS):
                        if s == 1 and three:
                            m = n - 3
                            pe.wait_ge(fwd_ready, done(m))
                            pe.wait_ge(expd, done(m - 1))
                            nc.tensor.matmul(psM[:, 0:N], k.ident[:, :], fwd[:, q, :], start=True, stop=False)
                            nc.tensor.matmul(psM[:, 0:N], fwd[:, q, :], k.ident[:, :], start=False, stop=False)
                            nc.tensor.matmul(psM[:, 0:N], k.identb[:, :], k.negm[:, bass.ds(m * N, N)], start=False,
                                             stop=True).then_inc(m_mm, 1)
                        if s == 1 and four:
                            m = n - 4
                            pe.wait_ge(dg_ready, done(m))
                            pe.wait_ge(expd, done(m))
                            pe.wait_ge(y_ready, done(m - 1))
                            nc.tensor.matmul(psA[:, 0:N], ex[:, p, :], dg[:, p, :], start=True, stop=True).then_inc(att_mm, 1)
                        if zero:
                            product(n, s)
                        for slot, j in ((0, 1), (0, 2), (1, 3)):
                            if s == slot and one:
                                second((n - 1) * SLABS + j, j, n - 1)
                        if s == 3 and zero:
                            second(n * SLABS, 0, n)
                        if zero and s in LINEAR:
                            linear_part(n, s)
                        if s == 2 and one:
                            m = n - 1
                            pe.wait_ge(rows_ready, done(m))
                            pe.wait_ge(rot_ready, done(m - 1))
                            for d in range(4):
                                last = nc.tensor.transpose(psT[:, d * N:(d + 1) * N], rows[:, d * N:(d + 1) * N], k.ident[:, :])
                            last.then_inc(turned, 1)
                        if s == 3 and four:
                            m = n - 4
                            pe.wait_ge(att_ready, done(m))
                            pe.wait_ge(hg_ready, done(m))
                            nc.tensor.matmul(psA[:, 128:256], hg[:, p, :], attT[:, p, :], start=True, stop=True).then_inc(y_mm, 1)
                graphs(pe, step)


def phase_output(nc, k, hd, hy, ystats, out):
    with ExitStack() as ctx:
        sb = lambda name, shape, dt=F32: k.sb(ctx, "o_" + name, shape, dt)
        mv = sb("mv", [C, 2])
        v = sb("v", [C, 6])
        hq = sb("hq", [C, 2, QC])
        yn = sb("yn", [C, 2, QC])
        t1 = sb("t1", [N, 2, QC])
        res = sb("res", [N, 2, QC])
        psU = k.ps(ctx, "o_psU", [N, 2, 512])
        sem = lambda name: k.sem("o_" + name)
        algebra, rooted, scaled, leaky, h_copied, u_mm, biased, res_ready = (sem(n) for n in (
            "algebra", "rooted", "scaled", "leaky", "h_copied", "u_mm", "biased", "res_ready"))
        stored = [sem("stored0"), sem("stored1")]
        b = lambda i: slice(i * N, (i + 1) * N)

        def quads(eng, step):
            with eng.Fori(0, QUADS // 2) as t:
                for u in (0, 1):
                    step(2 * t + u, u, t)

        with nc.Block() as block:
            @block.vector
            def _(dve):
                for s in (leaky, biased, res_ready):
                    dve.sem_inc(s, BIAS)
                at = [0]

                def link(ins):
                    at[0] += 1
                    ins.then_inc(algebra, 1)
                    dve.wait_ge(algebra, at[0])
                c = lambda i: v[:, i:i + 1]
                gg, beg = k.pcol[:, 6:7], k.pcol[:, 7:8]
                link(nc.vector.bn_aggr(mv[:, :], ystats[:].rearrange("c b s -> c (b s)")))
                link(nc.vector.tensor_scalar(c(0), mv[:, 1:2], EPS, None, ALU.add))
                dve.wait_ge(rooted, 1)
                link(nc.vector.reciprocal(c(2), c(1)))
                link(nc.vector.tensor_tensor(c(3), c(2), gg, ALU.mult))
                link(nc.vector.tensor_tensor(c(4), mv[:, 0:1], c(3), ALU.mult))
                link(nc.vector.tensor_tensor(c(5), beg, c(4), ALU.subtract))

                def relu(g, p):
                    dve.wait_ge(scaled, done(g))
                    nc.vector.scalar_tensor_tensor(out=yn[:, p, :], in0=yn[:, p, :], scalar=0.01, in1=yn[:, p, :],
                                                   op0=ALU.mult, op1=ALU.max).then_inc(leaky, 1)

                def step(g, p, t, next=True):
                    if next:
                        relu(g + 1, 1 - p)
                    dve.wait_ge(u_mm, done(g))
                    dve.wait_ge(res_ready, done(g - 2))
                    nc.vector.tensor_tensor(
                        t1[:, p, :].rearrange("n (b c) -> n b c", c=C), psU[:, p, :].rearrange("n (b c) -> n b c", c=C),
                        k.bt[:, :].unsqueeze(1).broadcast_to([N, G, C]), ALU.add).then_inc(biased, 1)
                    dve.wait_ge(biased, done(g))
                    dve.wait_ge(stored[p], 16 * t + 16)
                    nc.vector.tensor_tensor(res[:, p, :], t1[:, p, :], k.x[:, bass.ds(g * QC, QC)], ALU.add).then_inc(res_ready, 1)
                relu(0, 0)
                with dve.Fori(0, QUADS // 2 - 1) as t:
                    for u in (0, 1):
                        step(2 * t + u, u, t)
                step(QUADS - 2, 0, QUADS // 2 - 1)
                step(QUADS - 1, 1, QUADS // 2 - 1, next=False)

            @block.gpsimd
            def _(pool):
                pool.sem_inc(h_copied, BIAS)

                def step(g, p, t):
                    pool.wait_ge(u_mm, done(g - 2))
                    nc.gpsimd.tensor_copy(
                        hq[:, p, :].rearrange("c (b n) -> c b n", n=N),
                        hd[:, bass.ds(g * (G * DUP), G * DUP)].rearrange("c (b n) -> c b n", n=DUP)[:, :, 0:N]).then_inc(h_copied, 1)
                quads(pool, step)

            @block.scalar
            def _(act):
                act.sem_inc(scaled, BIAS)
                act.wait_ge(algebra, 2)
                nc.scalar.activation(v[:, 1:2], v[:, 0:1], ACT.Sqrt).then_inc(rooted, 1)
                act.wait_ge(algebra, 6)

                def step(g, p, t):
                    act.wait_ge(u_mm, done(g - 2))
                    nc.scalar.activation(yn[:, p, :], hy[:, bass.ds(g * QC, QC)], ACT.Identity, bias=v[:, 5:6],
                                         scale=v[:, 3:4]).then_inc(scaled, 1)
                quads(act, step)

            @block.tensor
            def _(pe):
                pe.sem_inc(u_mm, BIAS)

                def step(g, p, t):
                    pe.wait_ge(h_copied, done(g))
                    pe.wait_ge(leaky, done(g))
                    pe.wait_ge(biased, done(g - 2))
                    for i in range(G):
                        nc.tensor.matmul(psU[:, p, b(i)], hq[:, p, b(i)], k.wtT[:, 0, :], start=True, stop=False)
                        last = nc.tensor.matmul(psU[:, p, b(i)], yn[:, p, b(i)], k.wtT[:, 1, :], start=False, stop=True)
                    last.then_inc(u_mm, 1)
                quads(pe, step)

            @block.sync
            def _(sp):
                for p in (0, 1):
                    sp.sem_inc(stored[p], 16)

                for g in range(QUADS):
                    sp.wait_ge(res_ready, done(g))
                    sp.dma_start(out[g * G:(g + 1) * G].rearrange("b n c -> n b c"),
                                 res[:, g % 2, :].rearrange("n (b c) -> n b c", c=C)).then_inc(stored[g % 2], 16)
                for p in (0, 1):
                    sp.wait_ge(stored[p], 16 * (QUADS // 2) + 16)


_INS = ['x', 'adj', 'nodemask', 'L0_gnn_W', 'L0_gnn_b', 'L0_gnn_a', 'L1_gnn_W1', 'L1_gnn_b1', 'L1_gnn_W2', 'L1_gnn_b2',
        'L1_gnn_Wu', 'L1_gnn_bu', 'L2_gnn_W', 'L2_gnn_a_w', 'L2_gnn_a_b', 'L3_gnn_W1', 'L3_gnn_b1', 'L3_gnn_g1',
        'L3_gnn_be1', 'L3_gnn_W2', 'L3_gnn_b2', 'L3_gnn_Wg', 'L3_gnn_bg', 'L3_gnn_gg', 'L3_gnn_beg', 'L3_gnn_Wt',
        'L3_gnn_bt']


def kernel(**inputs):
    import numpy as _np
    import concourse.bacc as _bacc
    from concourse import mybir as _mybir
    from concourse.bass_utils import run_bass_kernel_spmd as _run

    nc = _bacc.Bacc("TRN2", target_bir_lowering=False, num_devices=1)
    arrays, args = {}, {}
    given = {name: _np.ascontiguousarray(inputs[name]) for name in _INS}
    for name, v in {**given, **constants()}.items():
        arrays[f"in_{name}_dram"] = v
        args[name] = nc.dram_tensor(f"in_{name}_dram", v.shape, _mybir.dt.from_np(v.dtype), kind="ExternalInput").ap()
    out = nc.dram_tensor("out_0_dram", (B, N, C), _mybir.dt.float32, kind="ExternalOutput").ap()
    build(nc, args, out)
    r = _run(nc, [arrays], core_ids=[0])
    return r.results[0]["out_0_dram"]
```
